# Optimizing a Trainium2 kernel written in Bass

```python
import numpy as np
import jax
import jax.numpy as jnp

def _softmax(x, axis=-1):
    return jax.nn.softmax(x, axis=axis)

def _gelu(x):
    return jax.nn.gelu(x, approximate=True)

def _silu(x):
    return jax.nn.silu(x)

def _sigmoid(x):
    return jax.nn.sigmoid(x)

def _layernorm(x, axis=-1, eps=1e-05):
    m = jnp.mean(x, axis=axis, keepdims=True)
    v = jnp.var(x, axis=axis, keepdims=True)
    return (x - m) / jnp.sqrt(v + eps)

def _scatter_add(tgt, idx, src, axis=0):
    return tgt.at[idx].add(src)

def _segment_sum(src, seg, n):
    return jax.ops.segment_sum(src, seg, n)
kernel_name = 'mk_gnn_preln_d1_gnn_r32_46c8c8'

def setup_inputs(seed: int=0):
    np.random.seed(seed)
    _w = jnp.asarray

    def _rec_inputs():
        import jax
        import jax.numpy as jnp
        _gk = jax.random.key(seed)
        x = -0.000202 + 1 * jax.random.normal(jax.random.fold_in(_gk, 1), (3125, 128), jnp.float32)
        _s = jax.random.randint(jax.random.fold_in(_gk, 2), (25000,), 0, 3125, jnp.int32)
        _d = jax.random.randint(jax.random.fold_in(_gk, 3), (25000,), 0, 3125, jnp.int32)
        _loop = jnp.arange(3125, dtype=jnp.int32)
        src = jnp.concatenate([_s, _d, _loop])
        dst = jnp.concatenate([_d, _s, _loop])
        _o = jnp.argsort(dst, stable=True)
        src = src[_o]
        dst = dst[_o]
        edge_type_32 = jax.random.randint(jax.random.fold_in(_gk, 12), (53125,), 0, 32, jnp.int32)
        edge_weight = jax.random.uniform(jax.random.fold_in(_gk, 13), (53125,), jnp.float32, 0.0, 1)
        return (x, src, dst, edge_type_32, edge_weight)
    x, src, dst, edge_type_32, edge_weight = _rec_inputs()

    def _L0_gnn_setup():
        import jax, jax.numpy as jnp
        import numpy as np
        import math
        N_NODES = 50000
        N_EDGES = 50000
        IN_CH = 128
        OUT_CH = 128
        N_REL = 32
        key = jax.random.key(seed)
        k1, k2, k3, k4, k5, k6 = jax.random.split(key, 6)
        x = jax.random.normal(k1, (N_NODES, IN_CH), dtype=jnp.float32)
        edge_index = jax.random.randint(k2, (2, N_EDGES), 0, N_NODES, dtype=jnp.int64)
        edge_type = jax.random.randint(k3, (N_EDGES,), 0, N_REL, dtype=jnp.int64)
        edge_norm = jax.random.uniform(k4, (N_EDGES,), dtype=jnp.float32)
        stdv = 1.0 / math.sqrt(IN_CH)
        weight_relation = jax.random.uniform(k5, (N_REL, IN_CH, OUT_CH), dtype=jnp.float32, minval=-stdv, maxval=stdv)
        root = jax.random.uniform(k6, (IN_CH, OUT_CH), dtype=jnp.float32, minval=-stdv, maxval=stdv)
        return {'x': x, 'weight_relation': weight_relation, 'root': root, 'edge_index': edge_index, 'edge_type': edge_type, 'edge_norm': edge_norm, 'dim': N_NODES}
    _L0_gnn_all = _L0_gnn_setup()
    _L0_gnn_in = {k: v for k, v in _L0_gnn_all.items() if k in ('weight_relation', 'root')}
    del _L0_gnn_all
    return {'x': x, 'src': src, 'dst': dst, 'edge_type_32': edge_type_32, 'edge_weight': edge_weight, 'L0_gnn_weight_relation': _L0_gnn_in['weight_relation'], 'L0_gnn_root': _L0_gnn_in['root']}

def reference(x, src, dst, edge_type_32, edge_weight, L0_gnn_weight_relation, L0_gnn_root):
    import jax
    import jax.numpy as jnp

    def _L0_gnn_ref(x, weight_relation, root, edge_index, edge_type, edge_norm, dim):
        import jax, jax.numpy as jnp
        import numpy as np
        import math
        N_NODES = 50000
        N_EDGES = 50000
        IN_CH = 128
        OUT_CH = 128
        N_REL = 32
        h = jnp.einsum('nd,rdo->rno', x, weight_relation)
        src = edge_index[1]
        dst = edge_index[0]
        msg = h[edge_type, src]
        msg = msg * edge_norm[:, None]
        out = jax.ops.segment_sum(msg, dst, num_segments=dim)
        out = out + x @ root
        return out
    edge_index = jnp.stack([src, dst])
    h = jnp.maximum(_layernorm(x, axis=-1), 0.0)
    x = x + _L0_gnn_ref(h, L0_gnn_weight_relation, L0_gnn_root, edge_index, edge_type_32, edge_weight, 3125)
    return x

_drawn_inputs = setup_inputs


def setup_inputs(seed=0):
    import zlib

    import numpy as np

    out = dict(_drawn_inputs(seed))
    spreads = {}
    factors = {}
    for name, (base, spread) in spreads.items():
        noise = np.random.default_rng([zlib.crc32(name.encode()), seed]).standard_normal(out[name].shape)
        drawn = base * np.exp(spread * noise) if base else spread * noise
        out[name] = jnp.asarray(drawn.astype(out[name].dtype))
    for name, factor in factors.items():
        out[name] = (out[name] * factor).astype(out[name].dtype)
    return out
```

```python
import math

import numpy as np

import concourse.bass as bass
from concourse import mybir

F32 = mybir.dt.float32
F32R = mybir.dt.float32r
I32 = mybir.dt.int32
U32 = mybir.dt.uint32
ALU = mybir.AluOpType
ACT = mybir.ActivationFunctionType
AX = mybir.AxisListType

P = 128
NODES, FEAT, RELS, EDGES = 3125, 128, 32, 53125
EPS = 1e-5

GROUPS = -(-NODES // P)
FULL_GROUPS, TAIL_NODES = NODES // P, NODES % P
COLS = -(-EDGES // P)
SLOTS = 512
IN_ROWS = COLS * P // SLOTS
FULL_IN_ROWS, TAIL_EDGES = EDGES // SLOTS, EDGES % SLOTS
BLK = IN_ROWS
assert IN_ROWS * SLOTS == COLS * P and IN_ROWS - FULL_IN_ROWS == 1

ROW_BITS = 17
SEG_ONE = 4096
assert NODES * RELS < 2 ** ROW_BITS and NODES < SEG_ONE
KEY_BASE = 0x40000000
PAD_KEY = 1.7014118e38

SEG_TYPES = 8
FIRST_ROWS = NODES * SEG_TYPES
QUARTERS = RELS // SEG_TYPES
HALF = SEG_TYPES // 2 * FEAT
STAGE = 4
HBANKS = 4

BATCH = 4
BODY = 8
RING = 104
LAPS = COLS // RING
LAP_BODIES = RING // BODY
EARLY = 48
assert COLS == LAPS * RING and RING % BODY == 0 and BODY == 2 * BATCH
MRING, SRING = 4, 2
STATS_AT = 70


def group_cap():
    z, extra = 3.4, 1.0
    first = COLS * SEG_TYPES / RELS

    def node(c):
        c = min(max(c, 0.0), float(COLS))
        return c * NODES / first if c < first else NODES - (c - first) * NODES / (COLS - first)

    caps = []
    for b in range(0, COLS, BODY):
        span = 0.0
        for c in range(b, b + BODY):
            q = (c + 0.5) / COLS
            dev = z * math.sqrt(COLS * q * (1 - q)) + extra
            at = [node(c + 0.5 - dev), node(c + 0.5 + dev)]
            if c + 0.5 - dev < first < c + 0.5 + dev:
                at.append(float(NODES))
            span = max(span, max(at) - min(at))
        caps.append(min(GROUPS, int((span - 1) // P) + 2))
    return caps


def cap_runs():
    runs = []
    for b, cap in enumerate(group_cap()):
        if runs and runs[-1][2] == cap and b % LAP_BODIES:
            runs[-1][1] += 1
        else:
            runs.append([b, 1, cap])
    return runs


def build(nc, x, src, dst, edge_type, edge_weight, w_rel, root, out):
    table_rows = nc.dram_tensor("table", (NODES * RELS, FEAT), F32, kind="Internal").ap()
    first_rows = table_rows[0:FIRST_ROWS, :]
    first_table = first_rows.rearrange("(n r) f -> n (r f)", r=SEG_TYPES)
    second_table = table_rows[FIRST_ROWS:, :].rearrange("(n r) f -> n (r f)", r=RELS - SEG_TYPES)
    runs = cap_runs()
    WIDE = max(cap for _, _, cap in runs) * P
    PASS_GROUPS = 5
    PASSES = GROUPS // PASS_GROUPS
    assert PASSES * PASS_GROUPS == GROUPS and PASS_GROUPS * P <= WIDE

    from contextlib import ExitStack
    ctx = ExitStack()
    with ctx:
        def sb(name, shape, dt=F32):
            return ctx.enter_context(nc.sbuf_tensor(name, shape, dt))

        def sem(name):
            return ctx.enter_context(nc.semaphore(name))

        x_sb = sb("x_sb", [P, GROUPS, FEAT])
        iota = sb("iota", [P, WIDE])
        ident = sb("ident", [P, P])
        ones = sb("ones", [IN_ROWS, P])
        w_hi = sb("w_hi", [P, RELS * FEAT], F32R)
        w_lo = sb("w_lo", [P, RELS * FEAT], F32R)
        root_hi = sb("root_hi", [P, FEAT], F32R)
        root_lo = sb("root_lo", [P, FEAT], F32R)
        hT_hi = sb("hT_hi", [P, GROUPS * P], F32R)
        hT_lo = sb("hT_lo", [P, GROUPS * P], F32R)
        stage = sb("stage", [P, STAGE, 2 * HALF])
        key = sb("key", [P, 2, SLOTS])
        wgt = sb("wgt", [P, SLOTS])
        swap = sb("swap", [P, 2, SLOTS // 2], I32)
        kept = sb("kept", [P, SLOTS // 2])
        row_idx = sb("row_idx", [P, COLS], U32)
        ring_idx = sb("ring_idx", [P, RING], U32)
        src_abs = sb("src_abs", [P, COLS])
        src_rel = sb("src_rel", [P, COLS])
        seg_s = sb("seg_s", [P, COLS])
        tmp_i = sb("tmp_i", [P, COLS], I32)
        cap_row = sb("cap_row", [P, COLS])
        base = sb("base", [P, COLS])
        base_i = sb("base_i", [1, COLS], I32)
        over = sb("over", [P, COLS])
        edge_of = sb("edge_of", [IN_ROWS, 2 * COLS // BLK])
        edge_i = sb("edge_i", [IN_ROWS, 2 * COLS // BLK], I32)
        diag = sb("diag", [IN_ROWS, 2 * COLS // BLK, BLK])
        late = sb("late", [P, 2])
        late_i = sb("late_i", [1, 1], I32)
        long_f = sb("long_f", [1, 1])
        long_i = sb("long_i", [1, 1], I32)
        stats = sb("stats", [P, GROUPS, 6])
        mean_var = sb("mean_var", [P, GROUPS, 2])
        dev = sb("dev", [P, GROUPS])
        rstd = sb("rstd", [P, GROUPS])
        shift = sb("shift", [P, GROUPS])
        m_hi = sb("m_hi", [P, MRING, FEAT], F32R)
        m_lo = sb("m_lo", [P, MRING, FEAT], F32R)
        sel = sb("sel", [P, SRING, WIDE], F32R)
        ring = sb("ring", [P, RING * FEAT])
        rows = ring[:, :].rearrange("p (s f) -> p s f", f=FEAT)
        w_raw = ring[:, 0:RELS * FEAT]
        h_raw = ring[:, 4096:4096 + GROUPS * P].rearrange("p (g f) -> p g f", f=FEAT)
        hT_raw = ring[:, 7296:7296 + GROUPS * P]
        e_all = ring[:, 10496:10496 + 5 * SLOTS]
        e_w = e_all[0:IN_ROWS, 0:SLOTS]
        e_int = sb("e_int", [IN_ROWS, 3, SLOTS], I32)
        e_seg, e_turn, e_place = (e_all[0:IN_ROWS, (1 + i) * SLOTS:(2 + i) * SLOTS] for i in range(3))
        e_hi = sb("e_hi", [IN_ROWS, SLOTS], I32)
        e_low = sb("e_low", [IN_ROWS, SLOTS], I32)
        root_raw = e_all[:, 4 * SLOTS:4 * SLOTS + FEAT]

        psum = ctx.enter_context(nc.psum_tensor("psum", [P, 8, 512], F32))
        acc = psum[:, :, :].rearrange("p b c -> p (b c)")

        const_ready = sem("const_ready")
        pads_ready = sem("pads_ready")
        edges_in = sem("edges_in")
        x_in = sem("x_in")
        w_in = [sem(f"w_in{q}") for q in range(QUARTERS)]
        root_in = sem("root_in")
        key_step = sem("key_step")
        edges_t = sem("edges_t")
        sort_in = sem("sort_in")
        sort_step = sem("sort_step")
        ln_step = sem("ln_step")
        dev_ready = sem("dev_ready")
        h_ready = sem("h_ready")
        h_t = sem("h_t")
        hT_copied = sem("hT_copied")
        hT_hi_ready = sem("hT_hi_ready")
        hT_lo_ready = sem("hT_lo_ready")
        w_hi_ready = sem("w_hi_ready")
        w_lo_ready = sem("w_lo_ready")
        root_ready = sem("root_ready")
        prod_ready = sem("prod_ready")
        prod_copied = sem("prod_copied")
        stored = [sem(f"stored{s}") for s in range(STAGE)]
        decode = sem("decode")
        turn = sem("turn")
        late_seen = sem("late_seen")
        stat_step = sem("stat_step")
        bound = sem("bound")
        sel_ready = sem("sel_ready")
        lo_ready = sem("lo_ready")
        pass_summed = sem("pass_summed")
        src_t = sem("src_t")
        base_bc = sem("base_bc")
        base_ready = sem("base_ready")
        idx_ready = sem("idx_ready")
        gathered = [sem(f"gathered{k}") for k in range(2)]
        batch_begun = sem("batch_begun")
        hi_ready = sem("hi_ready")
        col_ready = sem("col_ready")
        col_summed = sem("col_summed")
        out_ready = sem("out_ready")
        out_stored = sem("out_stored")

        NSTEP = int(math.log2(SLOTS)) * (int(math.log2(SLOTS)) + 1) // 2
        SORT_OPS = 6
        LATE_STEP, IDX_STEP, SRC_STEP = 3, 1, 7
        CONSTS = 12
        UNITS = QUARTERS * GROUPS

        block = ctx.enter_context(nc.Block())

        @block.sync
        def _(sp):
            sp.wait_ge(pads_ready, 4)
            for i, a in enumerate((src, dst, edge_type)):
                sp.dma_start(e_int[0:FULL_IN_ROWS, i, :],
                             a[0:FULL_IN_ROWS * SLOTS].rearrange("(p c) -> p c", c=SLOTS)).then_inc(edges_in, 16)
                sp.dma_start(e_int[FULL_IN_ROWS:IN_ROWS, i, 0:TAIL_EDGES],
                             a[FULL_IN_ROWS * SLOTS:EDGES].rearrange("(p c) -> p c", p=1)).then_inc(edges_in, 16)
            sp.dma_start(e_w[0:FULL_IN_ROWS, :],
                         edge_weight[0:FULL_IN_ROWS * SLOTS].rearrange("(p c) -> p c", c=SLOTS)).then_inc(edges_in, 16)
            sp.dma_start(e_w[FULL_IN_ROWS:IN_ROWS, 0:TAIL_EDGES],
                         edge_weight[FULL_IN_ROWS * SLOTS:EDGES].rearrange("(p c) -> p c", p=1)).then_inc(edges_in, 16)
            for q in range(QUARTERS):
                sp.dma_start(w_raw[:, q * 2 * HALF:(q + 1) * 2 * HALF].rearrange("d (r o) -> d r o", o=FEAT),
                             w_rel[q * SEG_TYPES:(q + 1) * SEG_TYPES].rearrange("r d o -> d r o")).then_inc(w_in[q], 16)

            for u in range(UNITS):
                q, g = divmod(u, GROUPS)
                n = P if g < FULL_GROUPS else TAIL_NODES
                sp.wait_ge(prod_copied, 2 * u + 2)
                nodes = slice(g * P, g * P + n)
                sp.dma_start(second_table[nodes, (q - 1) * 2 * HALF:q * 2 * HALF] if q else first_table[nodes, :],
                             stage[0:n, u % STAGE, :]).then_inc(stored[u % STAGE], 16)
            for b in range(0, GROUPS, 4):
                sp.wait_ge(out_ready, b // 4 + 1)
                if b < FULL_GROUPS:
                    sp.dma_start(out[b * P:(b + 4) * P, :].rearrange("(g p) f -> p g f", p=P),
                                 x_sb[:, b:b + 4, :]).then_inc(out_stored, 16)
                else:
                    sp.dma_start(out[b * P:NODES, :], x_sb[0:TAIL_NODES, b, :]).then_inc(out_stored, 16)
            for s in range(STAGE):
                sp.wait_ge(stored[s], 16 * len(range(s, UNITS, STAGE)))
            sp.wait_ge(out_stored, 16 * -(-GROUPS // 4))

        @block.gpsimd
        def _(pool):
            nc.gpsimd.memset(ident[:], 0.0).then_inc(const_ready, 1)
            pool.wait_ge(const_ready, 1)
            nc.gpsimd.affine_select(out=ident[:], in_=ident[:], compare_op=ALU.not_equal, fill=1.0, base=0,
                                    pattern=[[-1, P]], channel_multiplier=1).then_inc(const_ready, 1)
            nc.gpsimd.memset(key[:, 0, COLS:SLOTS], PAD_KEY).then_inc(const_ready, 1)
            nc.gpsimd.memset(wgt[:, COLS:SLOTS], 0.0).then_inc(const_ready, 1)
            nc.gpsimd.memset(ones[:], 1.0).then_inc(const_ready, 1)
            nc.gpsimd.iota(iota[:], pattern=[[1, WIDE]], base=0, channel_multiplier=0,
                           allow_small_or_imprecise_dtypes=True).then_inc(const_ready, 1)
            for b, n, cap in runs:
                last = nc.gpsimd.memset(cap_row[:, b * BODY:(b + n) * BODY], float(cap))
            last.then_inc(const_ready, 1)

            def w_low(q):
                c = slice(q * 2 * HALF, (q + 1) * 2 * HALF)
                pool.wait_ge(w_hi_ready, q + 1)
                nc.gpsimd.tensor_tensor(w_lo[:, c], w_raw[:, c], w_hi[:, c], ALU.subtract).then_inc(w_lo_ready, 1)

            w_low(0)
            for c in range(-(-GROUPS // 4)):
                pool.wait_ge(hT_hi_ready, c + 1)
                s = slice(c * 512, min(GROUPS * P, (c + 1) * 512))
                nc.gpsimd.tensor_tensor(hT_lo[:, s], hT_raw[:, s], hT_hi[:, s], ALU.subtract).then_inc(hT_lo_ready, 1)
            for q in range(1, QUARTERS):
                w_low(q)
            pool.wait_ge(root_ready, 1)
            nc.gpsimd.tensor_tensor(root_lo[:], root_raw, root_hi[:], ALU.subtract).then_inc(root_ready, 1)

            pool.wait_ge(decode, LATE_STEP)
            nc.gpsimd.partition_all_reduce(late[:, 1:2], late[:, 0:1], P, bass.bass_isa.ReduceOp.max).then_inc(late_seen, 1)
            pool.wait_ge(late_seen, 1)
            nc.gpsimd.tensor_copy(late_i[:], late[0:1, 1:2]).then_inc(late_seen, 1)
            pool.wait_ge(late_seen, 2)
            is_late = pool.value_load(late_i[0:1, 0:1], min_val=0, max_val=1)

            def table_stored(units):
                for s in range(STAGE):
                    pool.wait_ge(stored[s], 16 * len(range(s, units, STAGE)))

            table_stored(GROUPS)
            pool.wait_ge(idx_ready, 1)
            pool.wait_ge(w_lo_ready, QUARTERS)
            pool.wait_ge(root_ready, 2)
            pool.wait_ge(h_t, -(-GROUPS // 4))
            pool.wait_ge(hT_lo_ready, -(-GROUPS // 4))

            def gather(b0, from_rows=table_rows):
                for s in range(b0 * BATCH, (b0 + 1) * BATCH):
                    nc.gpsimd.indirect_dma_start(
                        out=rows[:, s, :], out_offset=None, in_=from_rows,
                        in_offset=bass.IndirectOffsetOnAxis(ap=ring_idx[:, s:s + 1], axis=0),
                    ).then_inc(gathered[b0 % 2], 16)

            PER_LAP = RING // BATCH

            def first_lap(b, from_rows):
                if b >= 2:
                    pool.wait_ge(gathered[b % 2], 16 * BATCH * (b // 2))
                gather(b, from_rows)

            with pool.If(is_late > 0):
                table_stored(UNITS)
                for b in range(EARLY // BATCH):
                    first_lap(b, table_rows)
            with pool.Else():
                for b in range(EARLY // BATCH):
                    first_lap(b, first_rows)
            table_stored(UNITS)
            for b in range(EARLY // BATCH, PER_LAP):
                first_lap(b, table_rows)
            with pool.Fori(1, LAPS) as lap:
                for b in range(PER_LAP):
                    if b % 2 == 0:
                        pool.wait_ge(idx_ready, (lap - 1) * (RING // BODY) + b // 2 + 2)
                    pool.wait_ge(gathered[b % 2], lap * (16 * BATCH * PER_LAP // 2) + 16 * BATCH * (b // 2))
                    pool.sem_inc(batch_begun, 1)
                    gather(b)

        @block.scalar
        def _(act):
            act.wait_ge(pads_ready, 4)
            act.dma_start(x_sb[:, 0:FULL_GROUPS, :],
                          x[0:FULL_GROUPS * P, :].rearrange("(g p) f -> p g f", p=P)).then_inc(x_in, 16)
            act.dma_start(x_sb[0:TAIL_NODES, FULL_GROUPS, :], x[FULL_GROUPS * P:NODES, :]).then_inc(x_in, 16)
            act.dma_start(root_raw, root).then_inc(root_in, 16)

            def w_high(q):
                c = slice(q * 2 * HALF, (q + 1) * 2 * HALF)
                act.wait_ge(w_in[q], 16)
                nc.scalar.activation(w_hi[:, c], w_raw[:, c], ACT.Copy).then_inc(w_hi_ready, 1)

            w_high(0)
            act.wait_ge(ln_step, 1)
            nc.scalar.activation(dev[:], rstd[:], ACT.Sqrt).then_inc(dev_ready, 1)
            act.wait_ge(ln_step, 3)
            for g in range(GROUPS):
                nc.scalar.activation(h_raw[:, g, :], x_sb[:, g, :], ACT.Relu, bias=shift[:, g:g + 1],
                                     scale=rstd[:, g:g + 1]).then_inc(h_ready, 1)
            for c in range(-(-GROUPS // 4)):
                s = slice(c * 512, min(GROUPS * P, (c + 1) * 512))
                n = s.stop - s.start
                act.wait_ge(h_t, c + 1)
                nc.scalar.activation(hT_raw[:, s], psum[:, c % 4, 0:n], ACT.Copy).then_inc(hT_copied, 1)
                nc.scalar.activation(hT_hi[:, s], psum[:, c % 4, 0:n], ACT.Copy).then_inc(hT_hi_ready, 1)
            for q in range(1, QUARTERS):
                w_high(q)
            act.wait_ge(root_in, 16)
            nc.scalar.activation(root_hi[:], root_raw, ACT.Copy).then_inc(root_ready, 1)

            for u in range(UNITS):
                if u >= STAGE:
                    act.wait_ge(stored[u % STAGE], 16 * (u // STAGE))
                for k in range(2):
                    act.wait_ge(prod_ready, 2 * u + k + 1)
                    nc.scalar.activation(stage[:, u % STAGE, k * HALF:(k + 1) * HALF],
                                         psum[:, (2 * u + k) % HBANKS, 0:HALF], ACT.Copy).then_inc(prod_copied, 1)

            def high(t, slot, u, first):
                if u % BATCH == 0:
                    act.wait_ge(gathered[u // BATCH], t * (16 // 2) + (16 * BATCH))
                if not (first and u < MRING):
                    act.wait_ge(col_summed, t + (u - MRING + 1))
                nc.scalar.activation(m_hi[:, u % MRING, :], ring[:, bass.ds((slot + u) * FEAT, FEAT)],
                                     ACT.Copy, scale=wgt[:, bass.ds(t + u, 1)]).then_inc(hi_ready, 1)

            for u in range(BODY):
                high(0, 0, u, True)
            for lap in range(LAPS):
                with act.Fori(max(1, lap * LAP_BODIES), (lap + 1) * LAP_BODIES) as body:
                    for u in range(BODY):
                        high(body * BODY, (body - lap * LAP_BODIES) * BODY, u, False)

        @block.tensor
        def _(pe):
            pe.wait_ge(const_ready, 2)
            pe.wait_ge(key_step, 10)
            for b in range(COLS // BLK):
                last = nc.tensor.transpose(psum[:, 6, b * BLK:(b + 1) * BLK],
                                           e_hi[:, b * P:(b + 1) * P].bitcast(F32), ident[0:IN_ROWS, 0:IN_ROWS])
            last.then_inc(edges_t, 1)
            for b in range(COLS // BLK):
                last = nc.tensor.transpose(psum[:, 7, b * BLK:(b + 1) * BLK],
                                           e_w[:, b * P:(b + 1) * P], ident[0:IN_ROWS, 0:IN_ROWS])
            last.then_inc(edges_t, 1)
            for c in range(-(-GROUPS // 4)):
                if c >= 4:
                    pe.wait_ge(hT_hi_ready, c - 3)
                for g in range(4 * c, min(GROUPS, 4 * c + 4)):
                    pe.wait_ge(h_ready, g + 1)
                    last = nc.tensor.transpose(psum[:, c % 4, (g % 4) * P:(g % 4 + 1) * P], h_raw[:, g, :], ident[:])
                last.then_inc(h_t, 1)

            pe.wait_ge(hT_hi_ready, -(-GROUPS // 4))
            for u in range(UNITS):
                if u == STATS_AT:
                    pe.wait_ge(decode, SRC_STEP)
                    for b in range(COLS // BLK):
                        last = nc.tensor.transpose(psum[0:BLK, 6, b * P:(b + 1) * P],
                                                   src_abs[:, b * BLK:(b + 1) * BLK], ident[:])
                    last.then_inc(src_t, 1)
                if u == STATS_AT + 10:
                    pe.wait_ge(base_ready, 1)
                    for k in range(2 * COLS // BLK):
                        last = nc.tensor.matmul(psum[:, 4 + k // 4, (k % 4) * BLK:(k % 4 + 1) * BLK],
                                                ones[:], diag[:, k, :], start=True, stop=True)
                    last.then_inc(base_bc, 1)
                q, g = divmod(u, GROUPS)
                pe.wait_ge(w_hi_ready, q + 1)
                pe.wait_ge(w_lo_ready, q + 1)
                pe.wait_ge(hT_lo_ready, g // 4 + 1)
                for k in range(2):
                    n = 2 * u + k
                    if n >= HBANKS:
                        pe.wait_ge(prod_copied, n - HBANKS + 1)
                    cols = slice((2 * q + k) * HALF, (2 * q + k + 1) * HALF)
                    bank = psum[:, n % HBANKS, 0:HALF]
                    nodes = slice(g * P, (g + 1) * P)
                    nc.tensor.matmul(bank, hT_hi[:, nodes], w_hi[:, cols], start=True, stop=False)
                    nc.tensor.matmul(bank, hT_hi[:, nodes], w_lo[:, cols], start=False, stop=False)
                    nc.tensor.matmul(bank, hT_lo[:, nodes], w_hi[:, cols], start=False, stop=True).then_inc(prod_ready, 1)

            pe.wait_ge(prod_copied, 2 * UNITS)
            pe.wait_ge(root_ready, 2)
            pe.wait_ge(base_ready, 2)
            for g in range(GROUPS):
                a = acc[:, g * P:(g + 1) * P]
                nodes = slice(g * P, (g + 1) * P)
                nc.tensor.matmul(a, hT_hi[:, nodes], root_hi[:], start=(g % 4 == 0), stop=False, skip_group_check=True)
                nc.tensor.matmul(a, hT_hi[:, nodes], root_lo[:], start=False, stop=False, skip_group_check=True)
                nc.tensor.matmul(a, hT_lo[:, nodes], root_hi[:], start=False, stop=False, skip_group_check=True)

            def add(a, group, u, groups):
                for j in range(groups):
                    for part in (m_hi, m_lo):
                        last = nc.tensor.matmul(acc[:, bass.ds((group + j) * P, P)],
                                                sel[:, u % SRING, j * P:(j + 1) * P], part[:, u % MRING, :],
                                                start=False, stop=False, skip_group_check=True)
                return last

            is_long = pe.value_load(long_i[0:1, 0:1], min_val=0, max_val=1)
            with pe.If(is_long > 0):
                with pe.Fori(0, COLS // BODY) as body:
                    t = body * BODY
                    for u in range(BODY):
                        for p in range(PASSES):
                            pe.wait_ge(col_ready, (t + u) * PASSES + (p + 1))
                            for j in range(PASS_GROUPS):
                                for part in (m_hi, m_lo):
                                    last = nc.tensor.matmul(
                                        acc[:, (p * PASS_GROUPS + j) * P:(p * PASS_GROUPS + j + 1) * P],
                                        sel[:, (u * PASSES + p) % SRING, j * P:(j + 1) * P], part[:, u % MRING, :],
                                        start=False, stop=False, skip_group_check=True)
                            if p < PASSES - 1:
                                last.then_inc(pass_summed, 1)
                            else:
                                last.then_inc(col_summed, 1)
            with pe.Else():
                for b, n, cap in runs:
                    with pe.Fori(b, b + n) as body:
                        t = body * BODY
                        for u in range(BODY):
                            first = pe.value_load(base_i[0:1, bass.ds(t + u, 1)], min_val=0, max_val=GROUPS - cap)
                            pe.wait_ge(col_ready, t + (u + 1))
                            add(acc, first, u, cap).then_inc(col_summed, 1)

        @block.vector
        def _(dve):
            nc.vector.memset(e_int[96:IN_ROWS, 0:2, TAIL_EDGES:SLOTS], 0).then_inc(pads_ready, 1)
            nc.vector.memset(e_int[96:IN_ROWS, 2, TAIL_EDGES:SLOTS], RELS - 1).then_inc(pads_ready, 1)
            nc.vector.memset(e_w[96:IN_ROWS, TAIL_EDGES:SLOTS], 0.0).then_inc(pads_ready, 1)
            nc.vector.memset(x_sb[:, FULL_GROUPS, :], 0.0).then_inc(pads_ready, 1)
            dve.wait_ge(edges_in, 16 * 8)
            e_src, e_dst, e_typ = (e_int[:, i, :] for i in range(3))
            nc.vector.tensor_scalar(e_seg, e_typ, float(SEG_TYPES), None, ALU.is_ge).then_inc(key_step, 1)
            nc.vector.tensor_scalar(e_turn, e_src, -2.0, float(NODES - 1), ALU.mult, ALU.add).then_inc(key_step, 1)
            nc.vector.scalar_tensor_tensor(e_low[:], e_dst, float(SEG_TYPES), e_typ, ALU.mult, ALU.add).then_inc(key_step, 1)
            nc.vector.tensor_scalar(e_place, e_dst, float(RELS - 2 * SEG_TYPES), float(FIRST_ROWS - SEG_TYPES),
                                    ALU.mult, ALU.add).then_inc(key_step, 1)
            dve.wait_ge(key_step, 4)
            nc.vector.tensor_tensor(e_place, e_place, e_seg, ALU.mult).then_inc(key_step, 1)
            dve.wait_ge(key_step, 5)
            nc.vector.tensor_tensor(e_low[:], e_low[:], e_place, ALU.add).then_inc(key_step, 1)
            nc.vector.scalar_tensor_tensor(e_turn, e_turn, float(SEG_ONE), e_seg, ALU.add, ALU.mult).then_inc(key_step, 1)
            dve.wait_ge(key_step, 7)
            nc.vector.tensor_tensor(e_hi[:], e_src, e_turn, ALU.add).then_inc(key_step, 1)
            dve.wait_ge(key_step, 8)
            nc.vector.tensor_scalar(e_hi[:], e_hi[:], ROW_BITS, KEY_BASE, ALU.logical_shift_left,
                                    ALU.bitwise_or).then_inc(key_step, 1)
            dve.wait_ge(key_step, 9)
            nc.vector.tensor_tensor(e_hi[:], e_hi[:], e_low[:], ALU.bitwise_or).then_inc(key_step, 1)
            dve.wait_ge(x_in, 32)
            for g in range(GROUPS):
                nc.vector.bn_stats(stats[:, g, :], x_sb[:, g, :]).then_inc(stat_step, 1)
            for g in range(GROUPS):
                dve.wait_ge(stat_step, g + 1)
                last = nc.vector.bn_aggr(mean_var[:, g, :], stats[:, g, :])
            last.then_inc(stat_step, 1)
            dve.wait_ge(stat_step, GROUPS + 1)
            nc.vector.tensor_scalar(rstd[:], mean_var[:, :, 1], EPS, None, ALU.add).then_inc(ln_step, 1)
            dve.wait_ge(const_ready, 4)
            dve.wait_ge(edges_t, 1)
            nc.vector.tensor_copy(key[:, 0, 0:COLS], psum[:, 6, 0:COLS]).then_inc(sort_in, 1)
            dve.wait_ge(edges_t, 2)
            nc.vector.tensor_copy(wgt[:, 0:COLS], psum[:, 7, 0:COLS]).then_inc(sort_in, 1)
            dve.wait_ge(dev_ready, 1)
            nc.vector.reciprocal(rstd[:], dev[:]).then_inc(ln_step, 1)
            dve.wait_ge(ln_step, 2)
            nc.vector.scalar_tensor_tensor(shift[:], mean_var[:, :, 0], -1.0, rstd[:], ALU.mult,
                                           ALU.mult).then_inc(ln_step, 1)

            dve.wait_ge(sort_in, 2)
            step = 0
            for m in range(1, int(math.log2(SLOTS)) + 1):
                for d in range(m - 1, -1, -1):
                    h = 2 ** d
                    mirror = d == m - 1
                    now, new = key[:, step % 2, :], key[:, (step + 1) % 2, :]

                    def halves(v):
                        v = v.rearrange("p (b c) -> p b c", c=2 * h)
                        return v[:, :, 0:h], (v[:, :, 2 * h - 1:h - 1:-1] if mirror else v[:, :, h:2 * h])

                    (ka, kb), (na, nb), (wa, wb) = halves(now), halves(new), halves(wgt[:, :])
                    sw = swap[:, step % 2, :].rearrange("p (b c) -> p b c", c=h)
                    kp = kept[:, :].rearrange("p (b c) -> p b c", c=h)
                    did = SORT_OPS * step
                    if step:
                        dve.wait_ge(sort_step, did - 1)
                    nc.vector.tensor_tensor(sw, ka, kb, ALU.is_gt).then_inc(sort_step, 1)
                    if step:
                        dve.wait_ge(sort_step, did)
                    nc.vector.tensor_copy(kp, wa).then_inc(sort_step, 1)
                    nc.vector.tensor_tensor(na, ka, kb, ALU.min).then_inc(sort_step, 1)
                    dve.wait_ge(sort_step, did + 2)
                    nc.vector.copy_predicated(wa, sw, wb).then_inc(sort_step, 1)
                    nc.vector.tensor_tensor(nb, ka, kb, ALU.max).then_inc(sort_step, 1)
                    dve.wait_ge(sort_step, did + 4)
                    nc.vector.copy_predicated(wb, sw, kp).then_inc(sort_step, 1)
                    step += 1
            assert step == NSTEP
            dve.wait_ge(sort_step, SORT_OPS * NSTEP)

            bits = key[:, NSTEP % 2, 0:COLS].bitcast(I32)
            ubits = key[:, NSTEP % 2, 0:COLS].bitcast(U32)
            nc.vector.tensor_scalar(row_idx[:], ubits, 2 ** ROW_BITS - 1, None, ALU.bitwise_and).then_inc(decode, 1)
            nc.vector.tensor_scalar(tmp_i[:], bits, ROW_BITS, 2 * SEG_ONE - 1, ALU.logical_shift_right,
                                    ALU.bitwise_and).then_inc(decode, 1)
            dve.wait_ge(decode, 2)
            nc.vector.tensor_scalar(late[:, 0:1], tmp_i[:, EARLY - 1:EARLY], float(SEG_ONE), None,
                                    ALU.is_ge).then_inc(decode, 1)
            nc.vector.tensor_copy(ring_idx[:], row_idx[:, 0:RING]).then_inc(idx_ready, 1)
            nc.vector.tensor_scalar(seg_s[:], tmp_i[:], float(SEG_ONE), None, ALU.is_ge).then_inc(decode, 1)
            dve.wait_ge(decode, 4)
            nc.vector.scalar_tensor_tensor(src_rel[:], seg_s[:], -float(SEG_ONE), tmp_i[:], ALU.mult,
                                           ALU.add).then_inc(decode, 1)
            dve.wait_ge(decode, 5)
            nc.vector.tensor_scalar(over[:], src_rel[:], -2.0, float(NODES - 1), ALU.mult, ALU.add).then_inc(decode, 1)
            dve.wait_ge(decode, 6)
            nc.vector.tensor_tensor(over[:], over[:], seg_s[:], ALU.mult).then_inc(turn, 1)
            dve.wait_ge(turn, 1)
            nc.vector.tensor_tensor(src_abs[:], over[:], src_rel[:], ALU.add).then_inc(decode, 1)

            NB = COLS // BLK
            dve.wait_ge(src_t, 1)
            per_col = psum[0:BLK, 6, :].rearrange("p (b e) -> p b e", e=P)
            nc.vector.tensor_reduce(edge_of[:, 0:NB], per_col, AX.X, ALU.min).then_inc(bound, 1)
            nc.vector.tensor_reduce(edge_of[:, NB:2 * NB], per_col, AX.X, ALU.max).then_inc(bound, 1)
            dve.wait_ge(bound, 2)
            nc.vector.tensor_copy(edge_i[:], edge_of[:]).then_inc(bound, 1)
            dve.wait_ge(bound, 3)
            nc.vector.tensor_scalar(edge_i[:], edge_i[:], int(math.log2(P)), None, ALU.logical_shift_right).then_inc(bound, 1)
            dve.wait_ge(bound, 4)
            nc.vector.tensor_copy(edge_of[:], edge_i[:]).then_inc(bound, 1)
            dve.wait_ge(bound, 5)
            for k in range(2 * NB):
                last = nc.vector.tensor_scalar(diag[:, k, :], ident[0:BLK, 0:BLK], edge_of[:, k:k + 1], None, ALU.mult)
            last.then_inc(base_ready, 1)
            dve.wait_ge(base_bc, 1)
            dve.wait_ge(const_ready, 7)
            nc.vector.tensor_scalar(over[:], cap_row[:], -1.0, float(GROUPS), ALU.mult, ALU.add).then_inc(bound, 1)
            dve.wait_ge(bound, 6)
            nc.vector.tensor_tensor(base[:], over[:], psum[:, 4, 0:COLS], ALU.min).then_inc(bound, 1)
            dve.wait_ge(bound, 7)
            nc.vector.tensor_copy(base_i[:], base[0:1, :]).then_inc(bound, 1)
            nc.vector.scalar_tensor_tensor(src_rel[:], base[:], -float(P), src_abs[:], ALU.mult,
                                           ALU.add).then_inc(bound, 1)
            nc.vector.tensor_tensor(over[:], base[:], cap_row[:], ALU.add).then_inc(bound, 1)
            dve.wait_ge(bound, 10)
            nc.vector.scalar_tensor_tensor(over[:], over[:], -1.0, psum[:, 5, 0:COLS], ALU.mult,
                                           ALU.add).then_inc(bound, 1)
            dve.wait_ge(bound, 11)
            nc.vector.tensor_reduce(long_f[:], over[0:1, :], AX.X, ALU.max).then_inc(bound, 1)
            dve.wait_ge(bound, 12)
            nc.vector.tensor_scalar(long_i[:], long_f[:], 0.0, None, ALU.is_ge).then_inc(bound, 1)
            dve.wait_ge(bound, 13)
            nc.vector.memset(long_f[:], 0.0).then_inc(base_ready, 1)

            def low(t, slot, u):
                dve.wait_ge(hi_ready, t + (u + 1))
                if u % BATCH == 0:
                    dve.wait_ge(gathered[u // BATCH], t * (16 // 2) + (16 * BATCH))
                return nc.vector.scalar_tensor_tensor(
                    m_lo[:, u % MRING, :], ring[:, bass.ds((slot + u) * FEAT, FEAT)],
                    wgt[:, bass.ds(t + u, 1)], m_hi[:, u % MRING, :], ALU.mult, ALU.subtract)

            def next_rows(t, slot):
                nc.vector.tensor_copy(ring_idx[:, bass.ds(slot, BODY)],
                                      row_idx[:, bass.ds(t + RING, BODY)]).then_inc(idx_ready, 1)

            def short_col(t, slot, u, cap, first):
                if not (first and u < SRING):
                    dve.wait_ge(col_summed, t + (u - SRING + 1))
                nc.vector.tensor_scalar(sel[:, u % SRING, 0:cap * P], iota[:, 0:cap * P],
                                        src_rel[:, bass.ds(t + u, 1)], None, ALU.is_equal).then_inc(sel_ready, 1)
                low(t, slot, u).then_inc(col_ready, 1)

            is_long = dve.value_load(long_i[0:1, 0:1], min_val=0, max_val=1)
            with dve.If(is_long > 0):
                for lap in range(LAPS):
                    with dve.Fori(lap * LAP_BODIES, (lap + 1) * LAP_BODIES) as body:
                        t, slot = body * BODY, (body - lap * LAP_BODIES) * BODY
                        for u in range(BODY):
                            low(t, slot, u).then_inc(lo_ready, 1)
                            dve.wait_ge(lo_ready, t + (u + 1))
                            for p in range(PASSES):
                                nc.vector.tensor_scalar(sel[:, (u * PASSES + p) % SRING, 0:PASS_GROUPS * P],
                                                        iota[:, 0:PASS_GROUPS * P], float(p * PASS_GROUPS * P),
                                                        src_abs[:, bass.ds(t + u, 1)], ALU.add,
                                                        ALU.is_equal).then_inc(col_ready, 1)
                                if p < PASSES - 1:
                                    dve.wait_ge(pass_summed, (t + u) * (PASSES - 1) + (p + 1))
                                else:
                                    dve.wait_ge(col_summed, t + (u + 1))
                        if lap < LAPS - 1:
                            next_rows(t, slot)
            with dve.Else():
                for b, n, cap in runs:
                    lap = b // LAP_BODIES
                    start = b
                    if b == 0:
                        for u in range(BODY):
                            short_col(0, 0, u, cap, True)
                        next_rows(0, 0)
                        start = 1
                    if start < b + n:
                        with dve.Fori(start, b + n) as body:
                            t, slot = body * BODY, (body - lap * LAP_BODIES) * BODY
                            for u in range(BODY):
                                short_col(t, slot, u, cap, False)
                            if lap < LAPS - 1:
                                next_rows(t, slot)

            dve.wait_ge(col_summed, COLS)
            for b in range(0, GROUPS, 4):
                n = min(4, GROUPS - b)
                nc.vector.tensor_tensor(x_sb[:, b:b + n, :],
                                        acc[:, b * P:(b + n) * P].rearrange("p (g f) -> p g f", f=FEAT),
                                        x_sb[:, b:b + n, :], ALU.add).then_inc(out_ready, 1)


_INS = ["x", "src", "dst", "edge_type_32", "edge_weight", "L0_gnn_weight_relation", "L0_gnn_root"]


def kernel(**inputs):
    import concourse.bacc as bacc
    from concourse.bass_utils import run_bass_kernel_spmd as run

    nc = bacc.Bacc("TRN2", target_bir_lowering=False, num_devices=1)
    arrays, args = {}, []
    for name in _INS:
        a = np.ascontiguousarray(inputs[name])
        arrays[f"in_{name}"] = a
        args.append(nc.dram_tensor(f"in_{name}", a.shape, mybir.dt.from_np(a.dtype), kind="ExternalInput").ap())
    out = nc.dram_tensor("out_0", (NODES, FEAT), F32, kind="ExternalOutput").ap()
    build(nc, *args, out)
    return run(nc, [arrays], core_ids=[0]).results[0]["out_0"]
```

```python
import math

import numpy as np

import concourse.bass as bass
from concourse import mybir

F32 = mybir.dt.float32
F32R = mybir.dt.float32r
I32 = mybir.dt.int32
U32 = mybir.dt.uint32
ALU = mybir.AluOpType
ACT = mybir.ActivationFunctionType
AX = mybir.AxisListType

P = 128
NODES, FEAT, RELS, EDGES = 3125, 128, 32, 53125
EPS = 1e-5

GROUPS = -(-NODES // P)
FULL_GROUPS, TAIL_NODES = NODES // P, NODES % P
COLS = -(-EDGES // P)
SLOTS = 512
IN_ROWS = COLS * P // SLOTS
FULL_IN_ROWS, TAIL_EDGES = EDGES // SLOTS, EDGES % SLOTS
BLK = IN_ROWS
assert IN_ROWS * SLOTS == COLS * P and IN_ROWS - FULL_IN_ROWS == 1

ROW_BITS = 17
SEG_ONE = 4096
assert NODES * RELS < 2 ** ROW_BITS and NODES < SEG_ONE
KEY_BASE = 0x40000000
SECOND_KEY = float(2 ** 65)
PAD_KEY = 1.7014118e38

SEG_TYPES = 8
FIRST_ROWS = NODES * SEG_TYPES
QUARTERS = RELS // SEG_TYPES
BANK = 512
HALF = SEG_TYPES // 2 * FEAT
STAGE = 4
HBANK, HBANKS = 4, 4

BATCH = 4
BODY = 8
RING = 104
X_PARTS = 3
LAPS = COLS // RING
COPY_LAG, TURN_LAG, OUT_LAG = 2, 3, 5
SPARE = (7, 6)
LAP_BODIES = RING // BODY
EARLY = 72
assert COLS == LAPS * RING and RING % BODY == 0 and BODY == 2 * BATCH
MRING, SRING = 4, 2
FLAG_AT = 75
MISS = 1e-6


def windows():
    def at_most(c, q):
        a, b = math.log(q), math.log1p(-q)
        return sum(math.exp(math.lgamma(COLS + 1) - math.lgamma(k + 1) - math.lgamma(COLS - k + 1)
                            + k * a + (COLS - k) * b) for k in range(c + 1))

    top = []
    for c in range(COLS):
        low, high = 0.0, 1.0
        for _ in range(24):
            q = (low + high) / 2
            low, high = (q, high) if at_most(c, q) > MISS else (low, q)
        top.append(high)
    seam = SEG_TYPES / RELS

    def node(q):
        return NODES * (q / seam if q < seam else (1 - q) / (1 - seam))

    found = []
    for c in range(COLS):
        low, high = 1 - top[COLS - 1 - c], top[c]
        at = [node(low), node(high)] + ([float(NODES)] if low < seam < high else [])
        found.append((max(0, int(min(at))) // 2 * 2, min(NODES + 1, int(max(at)) // 2 * 2 + 2)))
    return found


def build(nc, x, src, dst, edge_type, edge_weight, w_rel, root, limits, out):
    table_rows = nc.dram_tensor("table", (NODES * RELS, FEAT), F32, kind="Internal").ap()
    first_rows = table_rows[0:FIRST_ROWS, :]
    first_table = first_rows.rearrange("(n r) f -> n (r f)", r=SEG_TYPES)
    second_table = table_rows[FIRST_ROWS:, :].rearrange("(n r) f -> n (r f)", r=RELS - SEG_TYPES)
    window = windows()
    WIDE = max(b - a for a, b in window)
    banks = [(b * BANK, min(GROUPS * P, (b + 1) * BANK)) for b in range(-(-GROUPS * P // BANK))]
    last_col = [max(c for c, (a, e) in enumerate(window) if a < hi and e > lo) for lo, hi in banks]
    done = sorted(range(len(banks)), key=lambda b: (last_col[b], -b))

    from contextlib import ExitStack
    ctx = ExitStack()
    with ctx:
        def sb(name, shape, dt=F32):
            return ctx.enter_context(nc.sbuf_tensor(name, shape, dt))

        def sem(name):
            return ctx.enter_context(nc.semaphore(name))

        x_sb = sb("x_sb", [P, GROUPS, FEAT])
        iota = sb("iota", [P, GROUPS * P])
        ident = sb("ident", [P, P])
        w_hi = sb("w_hi", [P, RELS * FEAT], F32R)
        w_lo = sb("w_lo", [P, RELS * FEAT], F32R)
        root_hi = sb("root_hi", [P, FEAT], F32R)
        root_lo = sb("root_lo", [P, FEAT], F32R)
        hT_hi = sb("hT_hi", [P, GROUPS * P], F32R)
        hT_lo = sb("hT_lo", [P, GROUPS * P], F32R)
        stage = sb("stage", [P, STAGE, 2 * HALF])
        key = sb("key", [P, 2, SLOTS])
        wgt = sb("wgt", [P, SLOTS])
        swap = sb("swap", [P, 2, SLOTS // 2], I32)
        kept = sb("kept", [P, SLOTS // 2])
        row_idx = sb("row_idx", [P, COLS], U32)
        ring_idx = sb("ring_idx", [P, RING], U32)
        src_abs = sb("src_abs", [P, COLS])
        seg_s = sb("seg_s", [P, COLS])
        place = sb("place", [P, COLS])
        turned = sb("turned", [P, COLS])
        tmp_i = sb("tmp_i", [P, COLS], I32)
        limit = sb("limit", [P, 2, COLS])
        late = sb("late", [P, 2])
        late_i = sb("late_i", [1, 1], I32)
        outside = sb("outside", [P, 1])
        long_f = sb("long_f", [1, 1])
        long_i = sb("long_i", [1, 1], I32)
        stats = sb("stats", [P, GROUPS, 6])
        mean_var = sb("mean_var", [P, GROUPS, 2])
        dev = sb("dev", [P, GROUPS])
        rstd = sb("rstd", [P, GROUPS])
        shift = sb("shift", [P, GROUPS])
        m_hi = sb("m_hi", [P, MRING, FEAT], F32R)
        m_lo = sb("m_lo", [P, MRING, FEAT], F32R)
        sel = sb("sel", [P, SRING, WIDE], F32R)
        ring = sb("ring", [P, RING * FEAT])
        rows = ring[:, :].rearrange("p (s f) -> p s f", f=FEAT)
        w_raw = ring[:, 0:RELS * FEAT]
        h_raw = ring[:, 4096:4096 + GROUPS * P].rearrange("p (g f) -> p g f", f=FEAT)
        hT_raw = ring[:, 7296:7296 + GROUPS * P]
        e_all = ring[:, 10496:10496 + 5 * SLOTS]
        e_w = e_all[0:IN_ROWS, 0:SLOTS]
        e_stage = stage[0:IN_ROWS, :, :].rearrange("p s c -> p (s c)").bitcast(I32)
        e_int = e_stage[:, 0:3 * SLOTS].rearrange("p (a c) -> p a c", c=SLOTS)
        e_seg, e_turn, e_place = (e_all[0:IN_ROWS, (1 + i) * SLOTS:(2 + i) * SLOTS] for i in range(3))
        e_hi = e_stage[:, 3 * SLOTS:4 * SLOTS]
        e_low = e_stage[:, 4 * SLOTS:5 * SLOTS]
        root_raw = e_all[:, 4 * SLOTS:4 * SLOTS + FEAT]

        psum = ctx.enter_context(nc.psum_tensor("psum", [P, 8, 512], F32))
        acc = psum[:, :, :].rearrange("p b c -> p (b c)")

        const_ready = sem("const_ready")
        pads_ready = sem("pads_ready")
        edges_in = sem("edges_in")
        weights_in = sem("weights_in")
        x_in = [sem(f"x_in{k}") for k in range(X_PARTS)]
        limit_in = sem("limit_in")
        w_in = [sem(f"w_in{q}") for q in range(QUARTERS)]
        root_in = sem("root_in")
        key_step = sem("key_step")
        edges_t = sem("edges_t")
        sort_in = sem("sort_in")
        sort_step = sem("sort_step")
        ln_step = sem("ln_step")
        dev_ready = sem("dev_ready")
        h_ready = sem("h_ready")
        h_t = sem("h_t")
        hT_copied = sem("hT_copied")
        hT_hi_ready = sem("hT_hi_ready")
        hT_lo_ready = sem("hT_lo_ready")
        w_hi_ready = sem("w_hi_ready")
        w_lo_ready = sem("w_lo_ready")
        root_ready = sem("root_ready")
        prod_ready = sem("prod_ready")
        prod_copied = sem("prod_copied")
        stored = [sem(f"stored{s}") for s in range(STAGE)]
        late_ready = sem("late_ready")
        decode = sem("decode")
        turn = sem("turn")
        late_seen = sem("late_seen")
        stat_step = sem("stat_step")
        check = sem("check")
        sel_ready = sem("sel_ready")
        pass_summed = sem("pass_summed")
        outside_t = sem("outside_t")
        long_ready = sem("long_ready")
        sums_copied = sem("sums_copied")
        sums_turned = sem("sums_turned")
        idx_ready = sem("idx_ready")
        gathered = [sem(f"gathered{k}") for k in range(2)]
        batch_begun = sem("batch_begun")
        hi_ready = sem("hi_ready")
        col_ready = sem("col_ready")
        col_summed = sem("col_summed")
        out_ready = sem("out_ready")
        out_stored = sem("out_stored")

        CHECKED = 4
        NSTEP = int(math.log2(SLOTS)) * (int(math.log2(SLOTS)) + 1) // 2
        SORT_OPS = 6
        UNITS = QUARTERS * GROUPS

        block = ctx.enter_context(nc.Block())

        @block.sync
        def _(sp):
            sp.wait_ge(pads_ready, 3)
            for i, a in enumerate((src, dst, edge_type)):
                sp.dma_start(e_int[0:FULL_IN_ROWS, i, :],
                             a[0:FULL_IN_ROWS * SLOTS].rearrange("(p c) -> p c", c=SLOTS)).then_inc(edges_in, 16)
                sp.dma_start(e_int[FULL_IN_ROWS:IN_ROWS, i, 0:TAIL_EDGES],
                             a[FULL_IN_ROWS * SLOTS:EDGES].rearrange("(p c) -> p c", p=1)).then_inc(edges_in, 16)
            sp.dma_start(e_w[0:FULL_IN_ROWS, :],
                         edge_weight[0:FULL_IN_ROWS * SLOTS].rearrange("(p c) -> p c", c=SLOTS)).then_inc(weights_in, 16)
            sp.dma_start(e_w[FULL_IN_ROWS:IN_ROWS, 0:TAIL_EDGES],
                         edge_weight[FULL_IN_ROWS * SLOTS:EDGES].rearrange("(p c) -> p c", p=1)).then_inc(weights_in, 16)
            for q in range(QUARTERS):
                sp.dma_start(w_raw[:, q * 2 * HALF:(q + 1) * 2 * HALF].rearrange("d (r o) -> d r o", o=FEAT),
                             w_rel[q * SEG_TYPES:(q + 1) * SEG_TYPES].rearrange("r d o -> d r o")).then_inc(w_in[q], 16)

            for u in range(UNITS):
                q, g = divmod(u, GROUPS)
                n = P if g < FULL_GROUPS else TAIL_NODES
                sp.wait_ge(prod_copied, 2 * u + 2)
                nodes = slice(g * P, g * P + n)
                sp.dma_start(second_table[nodes, (q - 1) * 2 * HALF:q * 2 * HALF] if q else first_table[nodes, :],
                             stage[0:n, u % STAGE, :]).then_inc(stored[u % STAGE], 16)
            for k, b in enumerate(done):
                g = b * BANK // P
                sp.wait_ge(out_ready, k + 1)
                if g < FULL_GROUPS:
                    sp.dma_start(out[g * P:(g + 4) * P, :].rearrange("(g p) f -> p g f", p=P),
                                 x_sb[:, g:g + 4, :]).then_inc(out_stored, 16)
                else:
                    sp.dma_start(out[g * P:NODES, :], x_sb[0:TAIL_NODES, g, :]).then_inc(out_stored, 16)
            for s in range(STAGE):
                sp.wait_ge(stored[s], 16 * len(range(s, UNITS, STAGE)))
            sp.wait_ge(out_stored, 16 * len(banks))

        @block.gpsimd
        def _(pool):
            nc.gpsimd.memset(ident[:], 0.0).then_inc(const_ready, 1)
            pool.wait_ge(const_ready, 1)
            nc.gpsimd.affine_select(out=ident[:], in_=ident[:], compare_op=ALU.not_equal, fill=1.0, base=0,
                                    pattern=[[-1, P]], channel_multiplier=1).then_inc(const_ready, 1)
            nc.gpsimd.memset(key[:, :, COLS:SLOTS], PAD_KEY).then_inc(const_ready, 1)
            nc.gpsimd.memset(wgt[:, COLS:SLOTS], 0.0).then_inc(const_ready, 1)
            nc.gpsimd.iota(iota[:], pattern=[[1, GROUPS * P]], base=0, channel_multiplier=0,
                           allow_small_or_imprecise_dtypes=True).then_inc(const_ready, 1)

            def w_low(q):
                c = slice(q * 2 * HALF, (q + 1) * 2 * HALF)
                pool.wait_ge(w_hi_ready, q + 1)
                nc.gpsimd.tensor_tensor(w_lo[:, c], w_raw[:, c], w_hi[:, c], ALU.subtract).then_inc(w_lo_ready, 1)

            w_low(0)
            pool.wait_ge(ln_step, 3)
            for g in range(GROUPS):
                nc.gpsimd.tensor_scalar(h_raw[:, g, :], x_sb[:, g, :], rstd[:, g:g + 1], shift[:, g:g + 1],
                                        ALU.mult, ALU.add).then_inc(h_ready, 1)
            for c in range(-(-GROUPS // 4)):
                pool.wait_ge(hT_hi_ready, c + 1)
                s = slice(c * 512, min(GROUPS * P, (c + 1) * 512))
                nc.gpsimd.tensor_tensor(hT_lo[:, s], hT_raw[:, s], hT_hi[:, s], ALU.subtract).then_inc(hT_lo_ready, 1)
            for q in range(1, QUARTERS):
                w_low(q)
            pool.wait_ge(root_ready, 1)
            nc.gpsimd.tensor_tensor(root_lo[:], root_raw, root_hi[:], ALU.subtract).then_inc(root_ready, 1)

            pool.wait_ge(late_ready, 1)
            nc.gpsimd.partition_all_reduce(late[:, 1:2], late[:, 0:1], P, bass.bass_isa.ReduceOp.max).then_inc(late_seen, 1)
            pool.wait_ge(late_seen, 1)
            nc.gpsimd.tensor_copy(late_i[:], late[0:1, 1:2]).then_inc(late_seen, 1)
            pool.wait_ge(late_seen, 2)
            is_late = pool.value_load(late_i[0:1, 0:1], min_val=0, max_val=1)

            def table_stored(units):
                for s in range(STAGE):
                    pool.wait_ge(stored[s], 16 * len(range(s, units, STAGE)))

            table_stored(GROUPS)
            pool.wait_ge(idx_ready, 1)
            pool.wait_ge(w_lo_ready, QUARTERS)
            pool.wait_ge(root_ready, 2)
            pool.wait_ge(h_t, -(-GROUPS // 4))
            pool.wait_ge(hT_lo_ready, -(-GROUPS // 4))

            def gather(b0, from_rows=table_rows):
                for s in range(b0 * BATCH, (b0 + 1) * BATCH):
                    nc.gpsimd.indirect_dma_start(
                        out=rows[:, s, :], out_offset=None, in_=from_rows,
                        in_offset=bass.IndirectOffsetOnAxis(ap=ring_idx[:, s:s + 1], axis=0),
                    ).then_inc(gathered[b0 % 2], 16)

            PER_LAP = RING // BATCH

            def first_lap(b, from_rows):
                if b >= 2:
                    pool.wait_ge(gathered[b % 2], 16 * BATCH * (b // 2))
                gather(b, from_rows)

            with pool.If(is_late > 0):
                table_stored(UNITS)
                for b in range(EARLY // BATCH):
                    first_lap(b, table_rows)
            with pool.Else():
                for b in range(EARLY // BATCH):
                    first_lap(b, first_rows)
            table_stored(UNITS)
            for b in range(EARLY // BATCH, PER_LAP):
                first_lap(b, table_rows)
            with pool.Fori(1, LAPS) as lap:
                for b in range(PER_LAP):
                    if b % 2 == 0:
                        pool.wait_ge(idx_ready, (lap - 1) * (RING // BODY) + b // 2 + 2)
                    pool.wait_ge(gathered[b % 2], lap * (16 * BATCH * PER_LAP // 2) + 16 * BATCH * (b // 2))
                    pool.sem_inc(batch_begun, 1)
                    gather(b)

        @block.scalar
        def _(act):
            act.wait_ge(pads_ready, 4)
            per = FULL_GROUPS // X_PARTS
            for k in range(X_PARTS):
                act.dma_start(x_sb[:, k * per:(k + 1) * per, :],
                              x[k * per * P:(k + 1) * per * P, :].rearrange("(g p) f -> p g f", p=P)).then_inc(x_in[k], 16)
            act.dma_start(x_sb[0:TAIL_NODES, FULL_GROUPS, :], x[FULL_GROUPS * P:NODES, :]).then_inc(x_in[-1], 16)
            act.dma_start(root_raw, root).then_inc(root_in, 16)
            act.dma_start(limit[:], limits.partition_broadcast(P)).then_inc(limit_in, 16)

            def w_high(q):
                c = slice(q * 2 * HALF, (q + 1) * 2 * HALF)
                act.wait_ge(w_in[q], 16)
                nc.scalar.activation(w_hi[:, c], w_raw[:, c], ACT.Copy).then_inc(w_hi_ready, 1)

            w_high(0)
            act.wait_ge(ln_step, 1)
            nc.scalar.activation(dev[:], rstd[:], ACT.Sqrt).then_inc(dev_ready, 1)
            for c in range(-(-GROUPS // 4)):
                s = slice(c * 512, min(GROUPS * P, (c + 1) * 512))
                n = s.stop - s.start
                act.wait_ge(h_t, c + 1)
                nc.scalar.activation(hT_raw[:, s], psum[:, c % 4, 0:n], ACT.Relu).then_inc(hT_copied, 1)
                nc.scalar.activation(hT_hi[:, s], psum[:, c % 4, 0:n], ACT.Relu).then_inc(hT_hi_ready, 1)
            act.wait_ge(edges_t, 2)

            for u in range(UNITS):
                if u in (4, 8, 12):
                    w_high(u // 4)
                if u == 16:
                    act.wait_ge(root_in, 16)
                    nc.scalar.activation(root_hi[:], root_raw, ACT.Copy).then_inc(root_ready, 1)
                if u >= STAGE:
                    act.wait_ge(stored[u % STAGE], 16 * (u // STAGE))
                for k in range(2):
                    act.wait_ge(prod_ready, 2 * u + k + 1)
                    nc.scalar.activation(stage[:, u % STAGE, k * HALF:(k + 1) * HALF],
                                         psum[:, HBANK + (2 * u + k) % HBANKS, 0:HALF], ACT.Copy).then_inc(prod_copied, 1)

            def high(t, slot, u, first):
                if u % BATCH == 0:
                    act.wait_ge(gathered[u // BATCH], t * (16 // 2) + (16 * BATCH))
                if not (first and u < MRING):
                    act.wait_ge(col_summed, t + (u - MRING + 1))
                nc.scalar.activation(m_hi[:, u % MRING, :], ring[:, bass.ds((slot + u) * FEAT, FEAT)],
                                     ACT.Copy, scale=wgt[:, bass.ds(t + u, 1)]).then_inc(hi_ready, 1)

            for u in range(BODY):
                high(0, 0, u, True)
            for lap in range(LAPS):
                with act.Fori(max(1, lap * LAP_BODIES), (lap + 1) * LAP_BODIES) as body:
                    for u in range(BODY):
                        high(body * BODY, (body - lap * LAP_BODIES) * BODY, u, False)

        @block.tensor
        def _(pe):
            pe.wait_ge(const_ready, 2)
            pe.wait_ge(key_step, 10)
            for b in range(COLS // BLK):
                last = nc.tensor.transpose(psum[:, 6, b * BLK:(b + 1) * BLK],
                                           e_hi[:, b * P:(b + 1) * P].bitcast(F32), ident[0:IN_ROWS, 0:IN_ROWS])
            last.then_inc(edges_t, 1)
            pe.wait_ge(weights_in, 32)
            for b in range(COLS // BLK):
                last = nc.tensor.transpose(psum[:, 7, b * BLK:(b + 1) * BLK],
                                           e_w[:, b * P:(b + 1) * P], ident[0:IN_ROWS, 0:IN_ROWS])
            last.then_inc(edges_t, 1)
            for c in range(-(-GROUPS // 4)):
                if c >= 4:
                    pe.wait_ge(hT_hi_ready, c - 3)
                for g in range(4 * c, min(GROUPS, 4 * c + 4)):
                    pe.wait_ge(h_ready, g + 1)
                    last = nc.tensor.transpose(psum[:, c % 4, (g % 4) * P:(g % 4 + 1) * P], h_raw[:, g, :], ident[:])
                last.then_inc(h_t, 1)

            pe.wait_ge(sort_in, 2)
            for u in range(UNITS):
                if u == FLAG_AT:
                    pe.wait_ge(check, CHECKED)
                    nc.tensor.matmul(psum[0:1, 3, 0:P], outside[:], ident[:], start=True,
                                     stop=True).then_inc(outside_t, 1)
                q, g = divmod(u, GROUPS)
                pe.wait_ge(w_hi_ready, q + 1)
                pe.wait_ge(w_lo_ready, q + 1)
                pe.wait_ge(hT_lo_ready, g // 4 + 1)
                for k in range(2):
                    n = 2 * u + k
                    if n >= HBANKS:
                        pe.wait_ge(prod_copied, n - HBANKS + 1)
                    cols = slice((2 * q + k) * HALF, (2 * q + k + 1) * HALF)
                    bank = psum[:, HBANK + n % HBANKS, 0:HALF]
                    nodes = slice(g * P, (g + 1) * P)
                    nc.tensor.matmul(bank, hT_hi[:, nodes], w_hi[:, cols], start=True, stop=False)
                    nc.tensor.matmul(bank, hT_hi[:, nodes], w_lo[:, cols], start=False, stop=False)
                    nc.tensor.matmul(bank, hT_lo[:, nodes], w_hi[:, cols], start=False, stop=True).then_inc(prod_ready, 1)

            pe.wait_ge(prod_copied, 2 * UNITS)
            pe.wait_ge(root_ready, 2)
            pe.wait_ge(long_ready, 1)
            for lo, hi in banks:
                for k, (r, h) in enumerate(((root_hi, hT_hi), (root_lo, hT_hi), (root_hi, hT_lo))):
                    nc.tensor.matmul(acc[:, lo:hi], r[:], h[:, lo:hi], start=(k == 0), stop=False,
                                     skip_group_check=True)

            def add(lo, hi, slot, c):
                for part in (m_hi, m_lo):
                    for b_lo, b_hi in banks:
                        a, e = max(lo, b_lo), min(hi, b_hi)
                        if a < e:
                            last = nc.tensor.matmul(acc[:, a:e], part[:, c % MRING, :],
                                                    sel[:, slot, a - lo:e - lo],
                                                    start=False, stop=False, skip_group_check=True)
                return last

            def turn_bank(k):
                lo, hi = banks[done[k]]
                pe.wait_ge(sums_copied, k + 1)
                if k >= 2:
                    pe.wait_ge(out_ready, k - 1)
                for a in range(0, hi - lo, P):
                    last = nc.tensor.transpose(psum[:, SPARE[k % 2], a:a + P], stage[:, k % 2, a:a + P], ident[:])
                last.then_inc(sums_turned, 1)

            is_long = pe.value_load(long_i[0:1, 0:1], min_val=0, max_val=1)
            with pe.If(is_long > 0):
                with pe.Fori(0, COLS // BODY) as body:
                    for u in range(BODY):
                        for p, (lo, hi) in enumerate(banks):
                            n = u * len(banks) + p
                            pe.wait_ge(sel_ready, body * (BODY * len(banks)) + (n + 1))
                            add(lo, hi, n % SRING, u).then_inc(pass_summed, 1)
                        pe.sem_inc(col_summed, 1)
                for k in range(len(banks)):
                    turn_bank(k)
            with pe.Else():
                k = 0
                for c, (lo, hi) in enumerate(window):
                    pe.wait_ge(col_ready, c + 1)
                    add(lo, hi, c % SRING, c).then_inc(col_summed, 1)
                    while k < len(banks) and last_col[done[k]] + TURN_LAG <= c:
                        turn_bank(k)
                        k += 1
                for k in range(k, len(banks)):
                    turn_bank(k)

        @block.vector
        def _(dve):
            nc.vector.memset(e_int[96:IN_ROWS, 0:2, TAIL_EDGES:SLOTS], 0).then_inc(pads_ready, 1)
            nc.vector.memset(e_int[96:IN_ROWS, 2, TAIL_EDGES:SLOTS], RELS - 1).then_inc(pads_ready, 1)
            nc.vector.memset(e_w[96:IN_ROWS, TAIL_EDGES:SLOTS], 0.0).then_inc(pads_ready, 1)
            nc.vector.memset(x_sb[:, FULL_GROUPS, :], 0.0).then_inc(pads_ready, 1)
            dve.wait_ge(edges_in, 16 * 6)
            e_src, e_dst, e_typ = (e_int[:, i, :] for i in range(3))
            nc.vector.tensor_scalar(e_seg, e_typ, float(SEG_TYPES), None, ALU.is_ge).then_inc(key_step, 1)
            nc.vector.tensor_scalar(e_turn, e_src, -2.0, float(NODES - 1), ALU.mult, ALU.add).then_inc(key_step, 1)
            nc.vector.scalar_tensor_tensor(e_low[:], e_dst, float(SEG_TYPES), e_typ, ALU.mult, ALU.add).then_inc(key_step, 1)
            nc.vector.tensor_scalar(e_place, e_dst, float(RELS - 2 * SEG_TYPES), float(FIRST_ROWS - SEG_TYPES),
                                    ALU.mult, ALU.add).then_inc(key_step, 1)
            dve.wait_ge(key_step, 4)
            nc.vector.tensor_tensor(e_place, e_place, e_seg, ALU.mult).then_inc(key_step, 1)
            dve.wait_ge(key_step, 5)
            nc.vector.tensor_tensor(e_low[:], e_low[:], e_place, ALU.add).then_inc(key_step, 1)
            nc.vector.scalar_tensor_tensor(e_turn, e_turn, float(SEG_ONE), e_seg, ALU.add, ALU.mult).then_inc(key_step, 1)
            dve.wait_ge(key_step, 7)
            nc.vector.tensor_tensor(e_hi[:], e_src, e_turn, ALU.add).then_inc(key_step, 1)
            dve.wait_ge(key_step, 8)
            nc.vector.tensor_scalar(e_hi[:], e_hi[:], ROW_BITS, KEY_BASE, ALU.logical_shift_left,
                                    ALU.bitwise_or).then_inc(key_step, 1)
            dve.wait_ge(key_step, 9)
            nc.vector.tensor_tensor(e_hi[:], e_hi[:], e_low[:], ALU.bitwise_or).then_inc(key_step, 1)
            for g in range(GROUPS):
                k = min(g * X_PARTS // FULL_GROUPS, X_PARTS - 1)
                dve.wait_ge(x_in[k], 32 if k == X_PARTS - 1 else 16)
                nc.vector.bn_stats(stats[:, g, :], x_sb[:, g, :]).then_inc(stat_step, 1)
            for g in range(GROUPS):
                dve.wait_ge(stat_step, g + 1)
                last = nc.vector.bn_aggr(mean_var[:, g, :], stats[:, g, :])
            last.then_inc(stat_step, 1)
            dve.wait_ge(stat_step, GROUPS + 1)
            nc.vector.tensor_scalar(rstd[:], mean_var[:, :, 1], EPS, None, ALU.add).then_inc(ln_step, 1)
            dve.wait_ge(const_ready, 4)
            dve.wait_ge(edges_t, 1)
            nc.vector.tensor_copy(key[:, 0, 0:COLS], psum[:, 6, 0:COLS]).then_inc(sort_in, 1)
            dve.wait_ge(edges_t, 2)
            nc.vector.tensor_copy(wgt[:, 0:COLS], psum[:, 7, 0:COLS]).then_inc(sort_in, 1)
            dve.wait_ge(dev_ready, 1)
            nc.vector.reciprocal(rstd[:], dev[:]).then_inc(ln_step, 1)
            dve.wait_ge(ln_step, 2)
            nc.vector.scalar_tensor_tensor(shift[:], mean_var[:, :, 0], -1.0, rstd[:], ALU.mult,
                                           ALU.mult).then_inc(ln_step, 1)

            dve.wait_ge(sort_in, 2)
            step = 0
            for m in range(1, int(math.log2(SLOTS)) + 1):
                for d in range(m - 1, -1, -1):
                    h = 2 ** d
                    mirror = d == m - 1
                    now, new = key[:, step % 2, :], key[:, (step + 1) % 2, :]

                    width = COLS if COLS % (2 * h) == 0 else SLOTS

                    def halves(v):
                        v = v[:, 0:width].rearrange("p (b c) -> p b c", c=2 * h)
                        return v[:, :, 0:h], (v[:, :, 2 * h - 1:h - 1:-1] if mirror else v[:, :, h:2 * h])

                    (ka, kb), (na, nb), (wa, wb) = halves(now), halves(new), halves(wgt[:, :])
                    sw = swap[:, step % 2, 0:width // 2].rearrange("p (b c) -> p b c", c=h)
                    kp = kept[:, 0:width // 2].rearrange("p (b c) -> p b c", c=h)
                    did = SORT_OPS * step
                    if step:
                        dve.wait_ge(sort_step, did - 1)
                    nc.vector.tensor_tensor(sw, ka, kb, ALU.is_gt).then_inc(sort_step, 1)
                    if step:
                        dve.wait_ge(sort_step, did)
                    nc.vector.tensor_copy(kp, wa).then_inc(sort_step, 1)
                    nc.vector.tensor_tensor(na, ka, kb, ALU.min).then_inc(sort_step, 1)
                    dve.wait_ge(sort_step, did + 2)
                    nc.vector.copy_predicated(wa, sw, wb).then_inc(sort_step, 1)
                    nc.vector.tensor_tensor(nb, ka, kb, ALU.max).then_inc(sort_step, 1)
                    dve.wait_ge(sort_step, did + 4)
                    nc.vector.copy_predicated(wb, sw, kp).then_inc(sort_step, 1)
                    step += 1
            assert step == NSTEP
            dve.wait_ge(sort_step, SORT_OPS * NSTEP)

            final = key[:, NSTEP % 2, 0:COLS]
            nc.vector.tensor_scalar(late[:, 0:1], final[:, EARLY - 1:EARLY], SECOND_KEY, None,
                                    ALU.is_ge).then_inc(late_ready, 1)
            ubits, bits = final.bitcast(U32), final.bitcast(I32)
            nc.vector.tensor_scalar(ring_idx[:], ubits[:, 0:RING], 2 ** ROW_BITS - 1, None,
                                    ALU.bitwise_and).then_inc(idx_ready, 1)
            nc.vector.tensor_scalar(row_idx[:], ubits, 2 ** ROW_BITS - 1, None, ALU.bitwise_and).then_inc(decode, 1)
            nc.vector.tensor_scalar(tmp_i[:], bits, ROW_BITS, 2 * SEG_ONE - 1, ALU.logical_shift_right,
                                    ALU.bitwise_and).then_inc(decode, 1)
            dve.wait_ge(decode, 2)
            nc.vector.tensor_scalar(seg_s[:], tmp_i[:], float(SEG_ONE), None, ALU.is_ge).then_inc(decode, 1)
            dve.wait_ge(decode, 3)
            nc.vector.scalar_tensor_tensor(place[:], seg_s[:], -float(SEG_ONE), tmp_i[:], ALU.mult,
                                           ALU.add).then_inc(decode, 1)
            dve.wait_ge(decode, 4)
            nc.vector.tensor_scalar(turned[:], place[:], -2.0, float(NODES - 1), ALU.mult, ALU.add).then_inc(decode, 1)
            dve.wait_ge(decode, 5)
            nc.vector.tensor_tensor(turned[:], turned[:], seg_s[:], ALU.mult).then_inc(decode, 1)
            dve.wait_ge(decode, 6)
            nc.vector.tensor_tensor(src_abs[:], turned[:], place[:], ALU.add).then_inc(decode, 1)
            dve.wait_ge(decode, 7)

            dve.wait_ge(limit_in, 16)
            nc.vector.tensor_tensor(turned[:], limit[:, 0, :], src_abs[:], ALU.subtract).then_inc(check, 1)
            nc.vector.tensor_tensor(place[:], src_abs[:], limit[:, 1, :], ALU.subtract).then_inc(check, 1)
            dve.wait_ge(check, 2)
            nc.vector.tensor_tensor(turned[:], turned[:], place[:], ALU.max).then_inc(check, 1)
            dve.wait_ge(check, 3)
            nc.vector.tensor_reduce(outside[:], turned[:], AX.X, ALU.max).then_inc(check, 1)

            def low(t, slot, u):
                dve.wait_ge(hi_ready, t + (u + 1))
                if u % BATCH == 0:
                    dve.wait_ge(gathered[u // BATCH], t * (16 // 2) + (16 * BATCH))
                nc.vector.scalar_tensor_tensor(
                    m_lo[:, u % MRING, :], ring[:, bass.ds((slot + u) * FEAT, FEAT)],
                    wgt[:, bass.ds(t + u, 1)], m_hi[:, u % MRING, :], ALU.mult, ALU.subtract).then_inc(col_ready, 1)

            def select(c, slot, lo, hi):
                return nc.vector.tensor_scalar(sel[:, slot, 0:hi - lo], iota[:, lo:hi],
                                               src_abs[:, bass.ds(c, 1)], None, ALU.is_equal)

            def next_rows(t, slot):
                nc.vector.tensor_copy(ring_idx[:, bass.ds(slot, BODY)],
                                      row_idx[:, bass.ds(t + RING, BODY)]).then_inc(idx_ready, 1)

            def copy_bank(k):
                lo, hi = banks[done[k]]
                dve.wait_ge(col_summed, last_col[done[k]] + 1)
                if k >= 2:
                    dve.wait_ge(sums_turned, k - 1)
                nc.vector.tensor_copy(stage[:, k % 2, 0:hi - lo], acc[:, lo:hi]).then_inc(sums_copied, 1)

            def out_bank(k):
                lo, hi = banks[done[k]]
                dve.wait_ge(sums_turned, k + 1)
                xs = x_sb[:, lo // P:hi // P, :].rearrange("p g f -> p (g f)")
                nc.vector.tensor_tensor(xs, psum[:, SPARE[k % 2], 0:hi - lo], xs, ALU.add).then_inc(out_ready, 1)

            for s in range(2):
                dve.wait_ge(stored[s], 16 * len(range(s, UNITS, STAGE)))

            dve.wait_ge(outside_t, 1)
            nc.vector.tensor_reduce(long_f[:], psum[0:1, 3, 0:P], AX.X, ALU.max).then_inc(check, 1)
            dve.wait_ge(check, CHECKED + 1)
            nc.vector.tensor_scalar(long_i[:], long_f[:], 0.0, None, ALU.is_gt).then_inc(long_ready, 1)
            dve.wait_ge(long_ready, 1)

            is_long = dve.value_load(long_i[0:1, 0:1], min_val=0, max_val=1)
            with dve.If(is_long > 0):
                for lap in range(LAPS):
                    start = lap * LAP_BODIES

                    def long_body(body, first):
                        t, slot = body * BODY, (body - lap * LAP_BODIES) * BODY
                        for u in range(BODY):
                            low(t, slot, u)
                            for p, (lo, hi) in enumerate(banks):
                                n = u * len(banks) + p
                                if not (first and n < SRING):
                                    dve.wait_ge(pass_summed, body * (BODY * len(banks)) + (n - SRING + 1))
                                select(t + u, n % SRING, lo, hi).then_inc(sel_ready, 1)
                        if lap < LAPS - 1:
                            next_rows(t, slot)

                    if lap == 0:
                        long_body(0, True)
                        start = 1
                    with dve.Fori(start, (lap + 1) * LAP_BODIES) as body:
                        long_body(body, False)
                for k in range(len(banks)):
                    copy_bank(k)
                    out_bank(k)
            with dve.Else():
                copied = turned_out = 0
                for c, (lo, hi) in enumerate(window):
                    if c >= SRING:
                        dve.wait_ge(col_summed, c - SRING + 1)
                    select(c, c % SRING, lo, hi).then_inc(sel_ready, 1)
                    low(c // BODY * BODY, c // BODY * BODY % RING, c % BODY)
                    if c % BODY == BODY - 1 and c < COLS - RING:
                        next_rows(c - BODY + 1, (c - BODY + 1) % RING)
                    if copied < len(banks) and last_col[done[copied]] + COPY_LAG <= c:
                        copy_bank(copied)
                        copied += 1
                    if turned_out < copied and last_col[done[turned_out]] + OUT_LAG <= c:
                        out_bank(turned_out)
                        turned_out += 1
                for k in range(turned_out, len(banks)):
                    if k >= copied:
                        copy_bank(k)
                    out_bank(k)


_INS = ["x", "src", "dst", "edge_type_32", "edge_weight", "L0_gnn_weight_relation", "L0_gnn_root"]


def kernel(**inputs):
    import concourse.bacc as bacc
    from concourse.bass_utils import run_bass_kernel_spmd as run

    nc = bacc.Bacc("TRN2", target_bir_lowering=False, num_devices=1)
    arrays, args = {}, []
    for name in _INS:
        a = np.ascontiguousarray(inputs[name])
        arrays[f"in_{name}"] = a
        args.append(nc.dram_tensor(f"in_{name}", a.shape, mybir.dt.from_np(a.dtype), kind="ExternalInput").ap())
    arrays["limits"] = np.array([[lo for lo, _ in windows()], [hi - 1 for _, hi in windows()]], np.float32)
    args.append(nc.dram_tensor("limits", arrays["limits"].shape, F32, kind="ExternalInput").ap())
    out = nc.dram_tensor("out_0", (NODES, FEAT), F32, kind="ExternalOutput").ap()
    build(nc, *args, out)
    return run(nc, [arrays], core_ids=[0]).results[0]["out_0"]
```

```python
import math

import numpy as np

import concourse.bass as bass
from concourse import mybir

F32 = mybir.dt.float32
F32R = mybir.dt.float32r
I32 = mybir.dt.int32
U32 = mybir.dt.uint32
ALU = mybir.AluOpType
ACT = mybir.ActivationFunctionType
AX = mybir.AxisListType

P = 128
NODES, FEAT, RELS, EDGES = 3125, 128, 32, 53125
EPS = 1e-5

GROUPS = -(-NODES // P)
FULL_GROUPS, TAIL_NODES = NODES // P, NODES % P
COLS = -(-EDGES // P)
SLOTS = 512
IN_ROWS = COLS * P // SLOTS
FULL_IN_ROWS, TAIL_EDGES = EDGES // SLOTS, EDGES % SLOTS
FOUR, PART = 4, P // 4
BLK = IN_ROWS
assert IN_ROWS * SLOTS == COLS * P and IN_ROWS - FULL_IN_ROWS == 1

ROW_BITS = 17
SEG_ONE = 4096
assert NODES * RELS < 2 ** ROW_BITS and NODES < SEG_ONE
KEY_BASE = 0x40000000
SECOND_KEY = float(2 ** 65)
PAD_KEY = 1.7014118e38

SEG_TYPES = 12
FIRST_ROWS = NODES * SEG_TYPES
STEPS = ((0, 8), (8, 4), (12, 8), (20, 8), (28, 4))
STEP_TYPES = 8
BANK = 512
BANK_TYPES = BANK // FEAT
assert sum(n for _, n in STEPS) == RELS and all(n % BANK_TYPES == 0 for _, n in STEPS)
STAGE = 4
HBANK, HBANKS = 4, 4

BATCH = 4
BODY = 8
RING = 104
X_PARTS = 3
ACT_NORMS = 3
LAPS = COLS // RING
FIRST_COLS = 120
COPY_LAG, TURN_LAG, OUT_LAG = 2, 3, 5
SPARE = (7, 6)
LAP_BODIES = RING // BODY
assert COLS == LAPS * RING and RING % BODY == 0 and BODY == 2 * BATCH and (FIRST_COLS - RING) % BODY == 0
MRING, SRING = 8, 4
assert BODY % MRING == 0
ACT_EVERY, ACT_AHEAD = 4, 3
FLAG_AT = 57
RSTD_AT = 3
COPY_AHEAD = 2
SHARE = 4
MISS = 1e-6


def windows():
    n = COLS // FOUR
    k = np.arange(n + 1)
    ways = np.array([math.lgamma(n + 1) - math.lgamma(i + 1) - math.lgamma(n - i + 1) for i in k])
    shares = np.arange(1, 4096) / 4096
    at_most = []
    for q in shares:
        chances = np.ones(1)
        for rank in range(FOUR):
            p = sum(math.comb(FOUR, i) * q ** i * (1 - q) ** (FOUR - i) for i in range(rank + 1, FOUR + 1))
            chances = np.convolve(chances, np.exp(ways + k * math.log(p) + (n - k) * math.log(max(1 - p, 1e-300))))
        at_most.append(np.cumsum(chances))
    at_most = np.array(at_most)
    top = [float(shares[np.argmax(at_most[:, c] <= MISS)]) if at_most[-1, c] <= MISS else 1.0
           for c in range(COLS)]
    seam = SEG_TYPES / RELS

    def node(q):
        return NODES * (q / seam if q < seam else (1 - q) / (1 - seam))

    found = []
    for c in range(COLS):
        low, high = 1 - top[COLS - 1 - c], top[c]
        at = [node(low), node(high)] + ([float(NODES)] if low < seam < high else [])
        found.append((max(0, int(min(at))) // 2 * 2, min(NODES + 1, int(max(at)) // 2 * 2 + 2)))
    return found


def build(nc, x, src, dst, edge_type, edge_weight, w_rel, root, limits, out):
    table_rows = nc.dram_tensor("table", (NODES * RELS, FEAT), F32, kind="Internal").ap()
    first_rows = table_rows[0:FIRST_ROWS, :]
    first_table = first_rows.rearrange("(n r) f -> n (r f)", r=SEG_TYPES)
    second_table = table_rows[FIRST_ROWS:, :].rearrange("(n r) f -> n (r f)", r=RELS - SEG_TYPES)
    window = windows()
    units = [(t0, n, g) for t0, n in STEPS for g in range(GROUPS)]
    UNITS = len(units)
    FIRST_UNITS = GROUPS * sum(t0 < SEG_TYPES for t0, _ in STEPS)
    prods = [0]
    for _, n, _ in units:
        prods.append(prods[-1] + n // BANK_TYPES)
    WIDE = max([BANK] + [b - a for a, b in window])
    banks = [(b * BANK, min(GROUPS * P, (b + 1) * BANK)) for b in range(-(-GROUPS * P // BANK))]
    last_col = [max(c for c, (a, e) in enumerate(window) if a < hi and e > lo) for lo, hi in banks]
    done = sorted(range(len(banks)), key=lambda b: (last_col[b], -b))

    per = FULL_GROUPS // X_PARTS
    x_parts = [(k * per, (k + 1) * per if k < X_PARTS - 1 else GROUPS) for k in range(X_PARTS)]
    assert FULL_GROUPS % X_PARTS == 0
    act_groups = list(range(ACT_NORMS - 1, GROUPS, ACT_NORMS))
    early_col = {u: i for i, u in enumerate(
        u for u in range(FLAG_AT + COPY_AHEAD, UNITS) if units[u][1] < STEP_TYPES or u % SHARE)}
    EARLY = len(early_col)
    early_banks = [b for b in range(len(banks)) if b < HBANK]
    assert all(hi <= early_banks[-1] * BANK + BANK for _, hi in window[:EARLY])
    act_cols = list(range(EARLY + ACT_AHEAD, COLS, ACT_EVERY))
    dve_cols = [c for c in range(COLS) if c not in act_cols]

    from contextlib import ExitStack
    ctx = ExitStack()
    with ctx:
        def sb(name, shape, dt=F32):
            return ctx.enter_context(nc.sbuf_tensor(name, shape, dt))

        def sem(name):
            return ctx.enter_context(nc.semaphore(name))

        x_sb = sb("x_sb", [P, GROUPS, FEAT])
        iota = sb("iota", [P, GROUPS * P])
        ident = sb("ident", [P, P])
        w_hi = sb("w_hi", [P, RELS * FEAT], F32R)
        w_lo = sb("w_lo", [P, RELS * FEAT], F32R)
        root_hi = sb("root_hi", [P, FEAT], F32R)
        root_lo = sb("root_lo", [P, FEAT], F32R)
        hT_hi = sb("hT_hi", [P, GROUPS * P], F32R)
        hT_lo = sb("hT_lo", [P, GROUPS * P], F32R)
        stage = sb("stage", [P, STAGE, STEP_TYPES * FEAT])
        key = sb("key", [P, 2, SLOTS])
        wgt = sb("wgt", [P, SLOTS])
        swap = sb("swap", [P, 2, SLOTS // 2], I32)
        kept = sb("kept", [P, SLOTS // 2])
        row_idx = sb("row_idx", [P, COLS], U32)
        ring_idx = sb("ring_idx", [P, RING], U32)
        src_abs = sb("src_abs", [P, COLS])
        seg_s = sb("seg_s", [P, COLS])
        place = sb("place", [P, COLS])
        turned = sb("turned", [P, COLS])
        tmp_i = sb("tmp_i", [P, COLS], I32)
        limit = sb("limit", [P, 2, COLS])
        late = sb("late", [P, 2])
        late_i = sb("late_i", [1, 1], I32)
        outside = sb("outside", [P, 1])
        long_f = sb("long_f", [1, 1])
        long_i = sb("long_i", [1, 1], I32)
        less_mean = sb("less_mean", [P, GROUPS])
        squares = sb("squares", [P, GROUPS])
        eps = sb("eps", [P, 1])
        dev = sb("dev", [P, GROUPS])
        rstd = sb("rstd", [P, GROUPS])
        shift = sb("shift", [P, GROUPS])
        m_hi = sb("m_hi", [P, MRING, FEAT], F32R)
        m_lo = sb("m_lo", [P, MRING, FEAT], F32R)
        sel = sb("sel", [P, SRING, WIDE], F32R)
        act_sel = w_hi[:, 0:2 * WIDE].rearrange("p (s c) -> p s c", c=WIDE)
        dist = stage[:, 2:4, :].rearrange("p s c -> p (s c)")
        one = sb("one", [P, 1])
        ring = sb("ring", [P, RING * FEAT])
        rows = ring[:, :].rearrange("p (s f) -> p s f", f=FEAT)
        w_raw = ring[:, 0:RELS * FEAT]
        H_AT, HT_AT, E_AT = RELS * FEAT, RELS * FEAT + GROUPS * P, RELS * FEAT + 2 * GROUPS * P
        h_raw = ring[:, H_AT:HT_AT].rearrange("p (g f) -> p g f", f=FEAT)
        hT_raw = ring[:, HT_AT:E_AT]
        halves = hT_raw[:, 0:GROUPS * FEAT // 2].rearrange("p (g f) -> p g f", f=FEAT // 2)
        e_all = ring[:, E_AT:E_AT + 5 * SLOTS]
        e_w = e_all[0:IN_ROWS, 0:SLOTS]
        e_stage = stage[0:IN_ROWS, :, :].rearrange("p s c -> p (s c)").bitcast(I32)
        e_int = e_stage[:, 0:3 * SLOTS].rearrange("p (a c) -> p a c", c=SLOTS)
        e_seg, e_turn, e_place = (e_all[0:IN_ROWS, (1 + i) * SLOTS:(2 + i) * SLOTS] for i in range(3))
        e_hi = e_stage[:, 3 * SLOTS:4 * SLOTS]
        e_low = e_stage[:, 4 * SLOTS:5 * SLOTS]
        four_key = e_stage[:, 5 * SLOTS:8 * SLOTS].bitcast(F32)
        half_w, four_w = e_all[0:IN_ROWS, SLOTS:2 * SLOTS], e_all[0:IN_ROWS, 2 * SLOTS:4 * SLOTS]
        root_raw = e_all[:, 4 * SLOTS:4 * SLOTS + FEAT]

        psum = ctx.enter_context(nc.psum_tensor("psum", [P, 8, 512], F32))
        acc = psum[:, :, :].rearrange("p b c -> p (b c)")

        const_ready = sem("const_ready")
        pads_ready = sem("pads_ready")
        edges_in = sem("edges_in")
        weights_in = sem("weights_in")
        x_in = [sem(f"x_in{k}") for k in range(X_PARTS)]
        limit_in = sem("limit_in")
        w_in = [sem(f"w_in{q}") for q in range(len(STEPS))]
        root_in = sem("root_in")
        key_step = sem("key_step")
        four_step = sem("four_step")
        edges_t = sem("edges_t")
        sort_in = sem("sort_in")
        sort_step = sem("sort_step")
        mean_step = sem("mean_step")
        squared = sem("squared")
        rstd_ready = sem("rstd_ready")
        shift_ready = sem("shift_ready")
        dev_ready = sem("dev_ready")
        h_ready = sem("h_ready")
        h_act_ready = sem("h_act_ready")
        h_t = sem("h_t")
        hT_copied = sem("hT_copied")
        hT_hi_ready = sem("hT_hi_ready")
        hT_lo_ready = sem("hT_lo_ready")
        w_hi_ready = sem("w_hi_ready")
        w_lo_ready = sem("w_lo_ready")
        root_ready = sem("root_ready")
        prod_ready = sem("prod_ready")
        prod_copied = sem("prod_copied")
        stored = [sem(f"stored{s}") for s in range(STAGE)]
        late_ready = sem("late_ready")
        decode = sem("decode")
        late_seen = sem("late_seen")
        check = sem("check")
        sel_ready = sem("sel_ready")
        dist_ready = sem("dist_ready")
        act_sel_ready = sem("act_sel_ready")
        pass_summed = sem("pass_summed")
        outside_t = sem("outside_t")
        long_ready = sem("long_ready")
        sums_copied = sem("sums_copied")
        sums_turned = sem("sums_turned")
        idx_ready = sem("idx_ready")
        gathered = [sem(f"gathered{k}") for k in range(2)]
        batch_begun = sem("batch_begun")
        hi_ready = sem("hi_ready")
        col_ready = sem("col_ready")
        col_summed = sem("col_summed")
        out_ready = sem("out_ready")
        out_stored = sem("out_stored")

        CHECKED = 5
        NSTEP = int(math.log2(SLOTS)) * (int(math.log2(SLOTS)) + 1) // 2
        SORT_OPS, FOUR_OPS = 6, 7
        MEAN_STEPS = int(math.log2(FEAT)) + 1

        block = ctx.enter_context(nc.Block())

        @block.sync
        def _(sp):
            sp.wait_ge(pads_ready, 3)
            for i, a in enumerate((src, dst, edge_type)):
                sp.dma_start(e_int[0:FULL_IN_ROWS, i, :],
                             a[0:FULL_IN_ROWS * SLOTS].rearrange("(p c) -> p c", c=SLOTS)).then_inc(edges_in, 16)
            sp.wait_ge(pads_ready, 4)
            for k in range(X_PARTS):
                sp.dma_start(x_sb[:, k * per:(k + 1) * per, :],
                             x[k * per * P:(k + 1) * per * P, :].rearrange("(g p) f -> p g f", p=P)).then_inc(x_in[k], 16)
            sp.dma_start(x_sb[0:TAIL_NODES, FULL_GROUPS, :], x[FULL_GROUPS * P:NODES, :]).then_inc(x_in[-1], 16)
            for q, (t0, n) in enumerate(STEPS):
                sp.dma_start(w_raw[:, t0 * FEAT:(t0 + n) * FEAT].rearrange("d (r o) -> d r o", o=FEAT),
                             w_rel[t0:t0 + n].rearrange("r d o -> d r o")).then_inc(w_in[q], 16)

            for u, (t0, n, g) in enumerate(units):
                nodes = slice(g * P, min((g + 1) * P, NODES))
                table, t0 = (first_table, t0) if t0 < SEG_TYPES else (second_table, t0 - SEG_TYPES)
                sp.wait_ge(prod_copied, prods[u + 1])
                sp.dma_start(table[nodes, t0 * FEAT:(t0 + n) * FEAT],
                             stage[0:nodes.stop - nodes.start, u % STAGE, 0:n * FEAT]).then_inc(stored[u % STAGE], 16)
            for k, b in enumerate(done):
                g = b * BANK // P
                sp.wait_ge(out_ready, k + 1)
                if g < FULL_GROUPS:
                    sp.dma_start(out[g * P:(g + 4) * P, :].rearrange("(g p) f -> p g f", p=P),
                                 x_sb[:, g:g + 4, :]).then_inc(out_stored, 16)
                else:
                    sp.dma_start(out[g * P:NODES, :], x_sb[0:TAIL_NODES, g, :]).then_inc(out_stored, 16)
            for s in range(STAGE):
                sp.wait_ge(stored[s], 16 * len(range(s, UNITS, STAGE)))
            sp.wait_ge(out_stored, 16 * len(banks))

        @block.gpsimd
        def _(pool):
            nc.gpsimd.memset(ident[:], 0.0).then_inc(const_ready, 1)
            pool.wait_ge(const_ready, 1)
            nc.gpsimd.affine_select(out=ident[:], in_=ident[:], compare_op=ALU.not_equal, fill=1.0, base=0,
                                    pattern=[[-1, P]], channel_multiplier=1).then_inc(const_ready, 1)
            nc.gpsimd.memset(key[:, :, COLS:SLOTS], PAD_KEY).then_inc(const_ready, 1)
            nc.gpsimd.memset(wgt[:, COLS:SLOTS], 0.0).then_inc(const_ready, 1)
            nc.gpsimd.iota(iota[:], pattern=[[1, GROUPS * P]], base=0, channel_multiplier=0,
                           allow_small_or_imprecise_dtypes=True).then_inc(const_ready, 1)

            nc.gpsimd.memset(one[:], 1.0).then_inc(const_ready, 1)
            nc.gpsimd.memset(eps[:], EPS).then_inc(const_ready, 1)

            def w_low(q):
                c = slice(STEPS[q][0] * FEAT, sum(STEPS[q]) * FEAT)
                pool.wait_ge(w_hi_ready, q + 1)
                nc.gpsimd.tensor_tensor(w_lo[:, c], w_raw[:, c], w_hi[:, c], ALU.subtract).then_inc(w_lo_ready, 1)

            for k, (g0, g1) in enumerate(x_parts):
                pool.wait_ge(x_in[k], 32 if k == X_PARTS - 1 else 16)
                summed, did = x_sb[:, g0:g1, :], MEAN_STEPS * k
                for i in range(MEAN_STEPS - 1):
                    half = FEAT >> (i + 1)
                    if i:
                        pool.wait_ge(mean_step, did + i)
                    nc.gpsimd.tensor_tensor(halves[:, g0:g1, 0:half], summed[:, :, 0:half],
                                            summed[:, :, half:2 * half], ALU.add).then_inc(mean_step, 1)
                    summed = halves[:, g0:g1, :]
                pool.wait_ge(mean_step, did + MEAN_STEPS - 1)
                nc.gpsimd.tensor_scalar(less_mean[:, g0:g1], halves[:, g0:g1, 0], -1.0 / FEAT, None,
                                        ALU.mult).then_inc(mean_step, 1)
            w_low(0)
            pool.wait_ge(rstd_ready, 1)
            nc.gpsimd.tensor_tensor(shift[:], less_mean[:], rstd[:], ALU.mult).then_inc(shift_ready, 1)
            pool.wait_ge(shift_ready, 1)
            for g in range(GROUPS):
                if g in act_groups:
                    continue
                nc.gpsimd.tensor_scalar(h_raw[:, g, :], x_sb[:, g, :], rstd[:, g:g + 1], shift[:, g:g + 1],
                                        ALU.mult, ALU.add).then_inc(h_ready, 1)
            for c in range(-(-GROUPS // 4)):
                pool.wait_ge(hT_hi_ready, c + 1)
                s = slice(c * 512, min(GROUPS * P, (c + 1) * 512))
                nc.gpsimd.tensor_tensor(hT_lo[:, s], hT_raw[:, s], hT_hi[:, s], ALU.subtract).then_inc(hT_lo_ready, 1)
            for q in range(1, len(STEPS)):
                w_low(q)
            pool.wait_ge(root_ready, 1)
            nc.gpsimd.tensor_tensor(root_lo[:], root_raw, root_hi[:], ALU.subtract).then_inc(root_ready, 1)

            pool.wait_ge(late_ready, 1)
            nc.gpsimd.partition_all_reduce(late[:, 1:2], late[:, 0:1], P, bass.bass_isa.ReduceOp.max).then_inc(late_seen, 1)
            pool.wait_ge(late_seen, 1)
            nc.gpsimd.tensor_copy(late_i[:], late[0:1, 1:2]).then_inc(late_seen, 1)
            pool.wait_ge(late_seen, 2)
            is_late = pool.value_load(late_i[0:1, 0:1], min_val=0, max_val=1)

            def table_stored(units):
                for s in range(STAGE):
                    pool.wait_ge(stored[s], 16 * len(range(s, units, STAGE)))

            table_stored(FIRST_UNITS)
            pool.wait_ge(idx_ready, 1)
            pool.wait_ge(w_lo_ready, len(STEPS))
            pool.wait_ge(root_ready, 2)
            pool.wait_ge(h_t, -(-GROUPS // 4))
            pool.wait_ge(hT_lo_ready, -(-GROUPS // 4))

            def gather(b0, from_rows=table_rows):
                for s in range(b0 * BATCH, (b0 + 1) * BATCH):
                    nc.gpsimd.indirect_dma_start(
                        out=rows[:, s, :], out_offset=None, in_=from_rows,
                        in_offset=bass.IndirectOffsetOnAxis(ap=ring_idx[:, s:s + 1], axis=0),
                    ).then_inc(gathered[b0 % 2], 16)

            PER_LAP = RING // BATCH

            def first_lap(b, from_rows):
                if b >= 2:
                    pool.wait_ge(gathered[b % 2], 16 * BATCH * (b // 2))
                gather(b, from_rows)

            def later_lap(lap, b, from_rows=table_rows):
                if b % 2 == 0:
                    pool.wait_ge(idx_ready, (lap - 1) * (RING // BODY) + b // 2 + 2)
                pool.wait_ge(gathered[b % 2], lap * (16 * BATCH * PER_LAP // 2) + 16 * BATCH * (b // 2))
                pool.sem_inc(batch_begun, 1)
                gather(b, from_rows)

            def first_columns(from_rows):
                for b in range(PER_LAP):
                    first_lap(b, from_rows)
                for b in range((FIRST_COLS - RING) // BATCH):
                    later_lap(1, b, from_rows)

            with pool.If(is_late > 0):
                table_stored(UNITS)
                first_columns(table_rows)
            with pool.Else():
                first_columns(first_rows)
            table_stored(UNITS)
            for b in range((FIRST_COLS - RING) // BATCH, PER_LAP):
                later_lap(1, b)
            with pool.Fori(2, LAPS) as lap:
                for b in range(PER_LAP):
                    later_lap(lap, b)

        @block.scalar
        def _(act):
            act.wait_ge(pads_ready, 3)
            for i, a in enumerate((src, dst, edge_type)):
                act.dma_start(e_int[FULL_IN_ROWS:IN_ROWS, i, 0:TAIL_EDGES],
                              a[FULL_IN_ROWS * SLOTS:EDGES].rearrange("(p c) -> p c", p=1)).then_inc(edges_in, 16)
            act.dma_start(e_w[0:FULL_IN_ROWS, :],
                          edge_weight[0:FULL_IN_ROWS * SLOTS].rearrange("(p c) -> p c", c=SLOTS)).then_inc(weights_in, 16)
            act.dma_start(e_w[FULL_IN_ROWS:IN_ROWS, 0:TAIL_EDGES],
                          edge_weight[FULL_IN_ROWS * SLOTS:EDGES].rearrange("(p c) -> p c", p=1)).then_inc(weights_in, 16)
            act.dma_start(root_raw, root).then_inc(root_in, 16)
            act.dma_start(limit[:], limits.partition_broadcast(P)).then_inc(limit_in, 16)

            def w_high(q):
                c = slice(STEPS[q][0] * FEAT, sum(STEPS[q]) * FEAT)
                act.wait_ge(w_in[q], 16)
                nc.scalar.activation(w_hi[:, c], w_raw[:, c], ACT.Copy).then_inc(w_hi_ready, 1)

            for k, (g0, g1) in enumerate(x_parts):
                act.wait_ge(mean_step, MEAN_STEPS * (k + 1))
                for g in range(g0, g1):
                    nc.scalar.activation(h_raw[:, g, :], x_sb[:, g, :], ACT.Square, bias=less_mean[:, g:g + 1],
                                         accum_out=squares[:, g:g + 1]).then_inc(squared, 1)
                if k == X_PARTS - 2:
                    w_high(0)
            act.wait_ge(squared, GROUPS)
            act.wait_ge(const_ready, 7)
            nc.scalar.activation(dev[:], squares[:], ACT.Sqrt, scale=1.0 / FEAT, bias=eps[:]).then_inc(dev_ready, 1)
            act.wait_ge(rstd_ready, 1)
            act.wait_ge(shift_ready, 1)
            for g in act_groups:
                nc.scalar.activation(h_raw[:, g, :], x_sb[:, g, :], ACT.Identity, scale=rstd[:, g:g + 1],
                                     bias=shift[:, g:g + 1]).then_inc(h_act_ready, 1)
            for c in range(-(-GROUPS // 4)):
                s = slice(c * 512, min(GROUPS * P, (c + 1) * 512))
                n = s.stop - s.start
                act.wait_ge(h_t, c + 1)
                nc.scalar.activation(hT_raw[:, s], psum[:, c % 4, 0:n], ACT.Relu).then_inc(hT_copied, 1)
                nc.scalar.activation(hT_hi[:, s], psum[:, c % 4, 0:n], ACT.Relu).then_inc(hT_hi_ready, 1)
            act.wait_ge(edges_t, 2)

            def copy_unit(u):
                n = units[u][1]
                if u % 4 == 3 and u // 4 + 1 < len(STEPS):
                    w_high(u // 4 + 1)
                if u == 4 * len(STEPS) - 1:
                    act.wait_ge(root_in, 16)
                    nc.scalar.activation(root_hi[:], root_raw, ACT.Copy).then_inc(root_ready, 1)
                if u >= STAGE:
                    act.wait_ge(stored[u % STAGE], 16 * (u // STAGE))
                for k in range(n // BANK_TYPES):
                    act.wait_ge(prod_ready, prods[u] + k + 1)
                    nc.scalar.activation(stage[:, u % STAGE, k * BANK:(k + 1) * BANK],
                                         psum[:, HBANK + (prods[u] + k) % HBANKS, :], ACT.Copy).then_inc(prod_copied, 1)

            for u in range(FLAG_AT):
                copy_unit(u)

            def high(t, slot, u, first):
                if u % BATCH == 0:
                    act.wait_ge(gathered[u // BATCH], t * (16 // 2) + (16 * BATCH))
                if not (first and u < MRING):
                    act.wait_ge(col_summed, t + (u - MRING + 1))
                nc.scalar.activation(m_hi[:, u % MRING, :], ring[:, bass.ds((slot + u) * FEAT, FEAT)],
                                     ACT.Copy, scale=wgt[:, bass.ds(t + u, 1)]).then_inc(hi_ready, 1)

            def act_select(n):
                c = act_cols[n]
                lo, hi = window[c]
                if n >= 2:
                    act.wait_ge(col_summed, act_cols[n - 2] + 1)
                if n:
                    act.wait_ge(act_sel_ready, n)
                nc.scalar.activation(dist[:, 0:hi - lo], iota[:, lo:hi], ACT.Square, scale=-1.0,
                                     bias=src_abs[:, c:c + 1]).then_inc(dist_ready, 1)
                act.wait_ge(dist_ready, n + 1)
                nc.scalar.activation(act_sel[:, n % 2, 0:hi - lo], dist[:, 0:hi - lo], ACT.Relu, scale=-1.0,
                                     bias=one[:]).then_inc(act_sel_ready, 1)

            act.wait_ge(decode, 7)
            act.wait_ge(long_ready, 1)
            is_long = act.value_load(long_i[0:1, 0:1], min_val=0, max_val=1)
            with act.If(is_long > 0):
                for u in range(FLAG_AT, UNITS):
                    copy_unit(u)
                for u in range(BODY):
                    high(0, 0, u, True)
                for lap in range(LAPS):
                    with act.Fori(max(1, lap * LAP_BODIES), (lap + 1) * LAP_BODIES) as body:
                        for u in range(BODY):
                            high(body * BODY, (body - lap * LAP_BODIES) * BODY, u, False)
            with act.Else():
                def weigh(c):
                    t = c // BODY * BODY
                    high(t, t % RING, c % BODY, c < BODY)

                for u in range(FLAG_AT, UNITS):
                    copy_unit(u)
                    if u + COPY_AHEAD in early_col:
                        weigh(early_col[u + COPY_AHEAD])
                for k in (2, 3):
                    act.wait_ge(stored[k], 16 * len(range(k, UNITS, STAGE)))
                for c in range(EARLY, COLS):
                    weigh(c)
                    if c + ACT_AHEAD in act_cols:
                        act_select(act_cols.index(c + ACT_AHEAD))

        @block.tensor
        def _(pe):
            pe.wait_ge(const_ready, 2)
            def to_partitions(bank, edges):
                for b in range(COLS // BLK):
                    last = nc.tensor.transpose(psum[:, bank, b * BLK:(b + 1) * BLK],
                                               edges[:, b * P:(b + 1) * P], ident[0:IN_ROWS, 0:IN_ROWS])
                last.then_inc(edges_t, 1)

            pe.wait_ge(four_step, 3 * FOUR_OPS - 2)
            to_partitions(6, four_key)
            pe.wait_ge(four_step, 3 * FOUR_OPS)
            to_partitions(7, four_w)
            for c in range(-(-GROUPS // 4)):
                if c >= 4:
                    pe.wait_ge(hT_hi_ready, c - 3)
                for g in range(4 * c, min(GROUPS, 4 * c + 4)):
                    pe.wait_ge(h_ready, sum(i not in act_groups for i in range(g + 1)))
                    if g in act_groups:
                        pe.wait_ge(h_act_ready, act_groups.index(g) + 1)
                    last = nc.tensor.transpose(psum[:, c % 4, (g % 4) * P:(g % 4 + 1) * P], h_raw[:, g, :], ident[:])
                last.then_inc(h_t, 1)

            pe.wait_ge(sort_in, 2)
            def make_unit(u):
                t0, types, g = units[u]
                pe.wait_ge(w_lo_ready, u // GROUPS + 1)
                pe.wait_ge(hT_lo_ready, g // 4 + 1)
                nodes = slice(g * P, (g + 1) * P)
                for k in range(types // BANK_TYPES):
                    n = prods[u] + k
                    if n >= HBANKS:
                        pe.wait_ge(prod_copied, n - HBANKS + 1)
                    cols = slice(t0 * FEAT + k * BANK, t0 * FEAT + (k + 1) * BANK)
                    bank = psum[:, HBANK + n % HBANKS, :]
                    nc.tensor.matmul(bank, hT_hi[:, nodes], w_hi[:, cols], start=True, stop=False)
                    nc.tensor.matmul(bank, hT_hi[:, nodes], w_lo[:, cols], start=False, stop=False)
                    nc.tensor.matmul(bank, hT_lo[:, nodes], w_hi[:, cols], start=False, stop=True).then_inc(prod_ready, 1)

            for u in range(FLAG_AT):
                make_unit(u)
            pe.wait_ge(check, CHECKED)
            nc.tensor.matmul(psum[0:1, 3, 0:P], outside[:], ident[:], start=True, stop=True).then_inc(outside_t, 1)
            pe.wait_ge(root_ready, 2)
            pe.wait_ge(long_ready, 1)

            def start_sums(some):
                for lo, hi in (banks[b] for b in some):
                    for k, (r, h) in enumerate(((root_hi, hT_hi), (root_lo, hT_hi), (root_hi, hT_lo))):
                        nc.tensor.matmul(acc[:, lo:hi], r[:], h[:, lo:hi], start=(k == 0), stop=False,
                                         skip_group_check=True)

            start_sums(early_banks)

            def start_late_sums():
                pe.wait_ge(prod_copied, prods[UNITS])
                start_sums([b for b in range(len(banks)) if b not in early_banks])

            def add(lo, hi, chosen, c):
                for part in (m_hi, m_lo):
                    for b_lo, b_hi in banks:
                        a, e = max(lo, b_lo), min(hi, b_hi)
                        if a < e:
                            last = nc.tensor.matmul(acc[:, a:e], part[:, c % MRING, :],
                                                    chosen[:, a - lo:e - lo],
                                                    start=False, stop=False, skip_group_check=True)
                return last

            def turn_bank(k):
                lo, hi = banks[done[k]]
                pe.wait_ge(sums_copied, k + 1)
                if k >= 2:
                    pe.wait_ge(out_ready, k - 1)
                for a in range(0, hi - lo, P):
                    last = nc.tensor.transpose(psum[:, SPARE[k % 2], a:a + P], stage[:, k % 2, a:a + P], ident[:])
                last.then_inc(sums_turned, 1)

            is_long = pe.value_load(long_i[0:1, 0:1], min_val=0, max_val=1)
            with pe.If(is_long > 0):
                for u in range(FLAG_AT, UNITS):
                    make_unit(u)
                start_late_sums()
                with pe.Fori(0, COLS // BODY) as body:
                    for u in range(BODY):
                        for p, (lo, hi) in enumerate(banks):
                            n = u * len(banks) + p
                            pe.wait_ge(sel_ready, body * (BODY * len(banks)) + (n + 1))
                            add(lo, hi, sel[:, n % SRING, :], u).then_inc(pass_summed, 1)
                        pe.wait_ge(pass_summed, body * (BODY * len(banks)) + (u + 1) * len(banks))
                        pe.sem_inc(col_summed, 1)
                for k in range(len(banks)):
                    turn_bank(k)
            with pe.Else():
                def sum_column(c):
                    if c in act_cols:
                        n = act_cols.index(c)
                        pe.wait_ge(act_sel_ready, n + 1)
                        chosen = act_sel[:, n % 2, :]
                    else:
                        chosen = sel[:, dve_cols.index(c) % SRING, :]
                    pe.wait_ge(col_ready, c + 1)
                    add(*window[c], chosen, c).then_inc(col_summed, 1)

                for u in range(FLAG_AT, UNITS):
                    make_unit(u)
                    if u in early_col:
                        sum_column(early_col[u])
                start_late_sums()
                k = 0
                for c in range(EARLY, COLS):
                    sum_column(c)
                    while k < len(banks) and last_col[done[k]] + TURN_LAG <= c:
                        turn_bank(k)
                        k += 1
                for k in range(k, len(banks)):
                    turn_bank(k)

        @block.vector
        def _(dve):
            nc.vector.memset(e_int[96:IN_ROWS, 0:2, TAIL_EDGES:SLOTS], 0).then_inc(pads_ready, 1)
            nc.vector.memset(e_int[96:IN_ROWS, 2, TAIL_EDGES:SLOTS], RELS - 1).then_inc(pads_ready, 1)
            nc.vector.memset(e_w[96:IN_ROWS, TAIL_EDGES:SLOTS], 0.0).then_inc(pads_ready, 1)
            nc.vector.memset(x_sb[:, FULL_GROUPS, :], 0.0).then_inc(pads_ready, 1)
            dve.wait_ge(edges_in, 16 * 6)
            e_src, e_dst, e_typ = (e_int[:, i, :] for i in range(3))
            nc.vector.tensor_scalar(e_seg, e_typ, float(SEG_TYPES), None, ALU.is_ge).then_inc(key_step, 1)
            nc.vector.tensor_scalar(e_turn, e_src, -2.0, float(NODES - 1), ALU.mult, ALU.add).then_inc(key_step, 1)
            nc.vector.scalar_tensor_tensor(e_low[:], e_dst, float(SEG_TYPES), e_typ, ALU.mult, ALU.add).then_inc(key_step, 1)
            nc.vector.tensor_scalar(e_place, e_dst, float(RELS - 2 * SEG_TYPES), float(FIRST_ROWS - SEG_TYPES),
                                    ALU.mult, ALU.add).then_inc(key_step, 1)
            dve.wait_ge(key_step, 4)
            nc.vector.tensor_tensor(e_place, e_place, e_seg, ALU.mult).then_inc(key_step, 1)
            dve.wait_ge(key_step, 5)
            nc.vector.tensor_tensor(e_low[:], e_low[:], e_place, ALU.add).then_inc(key_step, 1)
            nc.vector.scalar_tensor_tensor(e_turn, e_turn, float(SEG_ONE), e_seg, ALU.add, ALU.mult).then_inc(key_step, 1)
            dve.wait_ge(key_step, 7)
            nc.vector.tensor_tensor(e_hi[:], e_src, e_turn, ALU.add).then_inc(key_step, 1)
            dve.wait_ge(key_step, 8)
            nc.vector.tensor_scalar(e_hi[:], e_hi[:], ROW_BITS, KEY_BASE, ALU.logical_shift_left,
                                    ALU.bitwise_or).then_inc(key_step, 1)
            dve.wait_ge(key_step, 9)
            nc.vector.tensor_tensor(e_hi[:], e_hi[:], e_low[:], ALU.bitwise_or).then_inc(key_step, 1)
            dve.wait_ge(key_step, 10)
            dve.wait_ge(weights_in, 32)
            in_key, in_w = e_hi.bitcast(F32), e_w

            def outer_inner(v, c):
                v = v[:, 0:SLOTS].rearrange("p (i u c) -> p i u c", u=4, c=c)
                return v[:, :, 0:4:3, :], v[:, :, 1:3, :]

            def in_two(v, c):
                v = v[:, 0:SLOTS].rearrange("p (i j h c) -> p i j h c", i=2, h=2, c=c)
                return v[:, :, :, 0, :], v[:, :, :, 1, :]

            def exchanged(v):
                lower = v[:, 0:18 * PART].rearrange("p (i u c) -> p i u c", u=9, c=PART)
                upper = v[:, PART:15 * PART].rearrange("p (i u c) -> p i u c", u=7, c=PART)
                return lower[:, :, 0:7:2, :], upper[:, :, 0:7:2, :]

            steps = (
                (outer_inner(in_key, PART), outer_inner(four_key, PART), outer_inner(in_w, PART), outer_inner(half_w, PART)),
                (in_two(four_key, 2 * PART), outer_inner(in_key, 2 * PART), in_two(half_w, 2 * PART), outer_inner(in_w, 2 * PART)),
                (in_two(in_key, PART), exchanged(four_key), in_two(in_w, PART), exchanged(four_w)))
            for i, ((ka, kb), (na, nb), (wa, wb), (va, vb)) in enumerate(steps):
                did = FOUR_OPS * i
                sw = swap[0:IN_ROWS, i % 2, :].rearrange("p (i u c) -> p i u c", i=ka.shape[1], c=ka.shape[3])
                if i:
                    dve.wait_ge(four_step, did)
                nc.vector.tensor_tensor(sw, ka, kb, ALU.is_gt).then_inc(four_step, 1)
                nc.vector.tensor_copy(va, wa).then_inc(four_step, 1)
                nc.vector.tensor_copy(vb, wb).then_inc(four_step, 1)
                nc.vector.tensor_tensor(na, ka, kb, ALU.min).then_inc(four_step, 1)
                nc.vector.tensor_tensor(nb, ka, kb, ALU.max).then_inc(four_step, 1)
                dve.wait_ge(four_step, did + 2)
                nc.vector.copy_predicated(va, sw, wb).then_inc(four_step, 1)
                dve.wait_ge(four_step, did + 3)
                nc.vector.copy_predicated(vb, sw, wa).then_inc(four_step, 1)
            dve.wait_ge(const_ready, 4)
            dve.wait_ge(edges_t, 1)
            nc.vector.tensor_copy(key[:, 0, 0:COLS], psum[:, 6, 0:COLS]).then_inc(sort_in, 1)
            dve.wait_ge(edges_t, 2)
            nc.vector.tensor_copy(wgt[:, 0:COLS], psum[:, 7, 0:COLS]).then_inc(sort_in, 1)
            dve.wait_ge(sort_in, 2)
            step = 0
            for m in range(1, int(math.log2(SLOTS)) + 1):
                for d in range(m - 1, -1, -1):
                    h = 2 ** d
                    mirror = d == m - 1
                    now, new = key[:, step % 2, :], key[:, (step + 1) % 2, :]

                    width = COLS if COLS % (2 * h) == 0 else SLOTS

                    def halves(v):
                        v = v[:, 0:width].rearrange("p (b c) -> p b c", c=2 * h)
                        return v[:, :, 0:h], (v[:, :, 2 * h - 1:h - 1:-1] if mirror else v[:, :, h:2 * h])

                    (ka, kb), (na, nb), (wa, wb) = halves(now), halves(new), halves(wgt[:, :])
                    sw = swap[:, step % 2, 0:width // 2].rearrange("p (b c) -> p b c", c=h)
                    kp = kept[:, 0:width // 2].rearrange("p (b c) -> p b c", c=h)
                    did = SORT_OPS * step
                    if step:
                        dve.wait_ge(sort_step, did - 1)
                    nc.vector.tensor_tensor(sw, ka, kb, ALU.is_gt).then_inc(sort_step, 1)
                    if step == RSTD_AT:
                        dve.wait_ge(dev_ready, 1)
                        nc.vector.reciprocal(rstd[:], dev[:]).then_inc(rstd_ready, 1)
                    if step:
                        dve.wait_ge(sort_step, did)
                    nc.vector.tensor_copy(kp, wa).then_inc(sort_step, 1)
                    nc.vector.tensor_tensor(na, ka, kb, ALU.min).then_inc(sort_step, 1)
                    dve.wait_ge(sort_step, did + 2)
                    nc.vector.copy_predicated(wa, sw, wb).then_inc(sort_step, 1)
                    nc.vector.tensor_tensor(nb, ka, kb, ALU.max).then_inc(sort_step, 1)
                    dve.wait_ge(sort_step, did + 4)
                    nc.vector.copy_predicated(wb, sw, kp).then_inc(sort_step, 1)
                    step += 1
            assert step == NSTEP
            dve.wait_ge(sort_step, SORT_OPS * NSTEP)

            final = key[:, NSTEP % 2, 0:COLS]
            nc.vector.tensor_scalar(late[:, 0:1], final[:, FIRST_COLS - 1:FIRST_COLS], SECOND_KEY, None,
                                    ALU.is_ge).then_inc(late_ready, 1)
            ubits, bits = final.bitcast(U32), final.bitcast(I32)
            nc.vector.tensor_scalar(ring_idx[:], ubits[:, 0:RING], 2 ** ROW_BITS - 1, None,
                                    ALU.bitwise_and).then_inc(idx_ready, 1)
            nc.vector.tensor_scalar(row_idx[:], ubits, 2 ** ROW_BITS - 1, None, ALU.bitwise_and).then_inc(decode, 1)
            nc.vector.tensor_scalar(tmp_i[:], bits, ROW_BITS, 2 * SEG_ONE - 1, ALU.logical_shift_right,
                                    ALU.bitwise_and).then_inc(decode, 1)
            dve.wait_ge(decode, 2)
            nc.vector.tensor_scalar(seg_s[:], tmp_i[:], float(SEG_ONE), None, ALU.is_ge).then_inc(decode, 1)
            dve.wait_ge(decode, 3)
            nc.vector.scalar_tensor_tensor(place[:], seg_s[:], -float(SEG_ONE), tmp_i[:], ALU.mult,
                                           ALU.add).then_inc(decode, 1)
            dve.wait_ge(decode, 4)
            nc.vector.tensor_scalar(turned[:], place[:], -2.0, float(NODES - 1), ALU.mult, ALU.add).then_inc(decode, 1)
            dve.wait_ge(decode, 5)
            nc.vector.tensor_tensor(turned[:], turned[:], seg_s[:], ALU.mult).then_inc(decode, 1)
            dve.wait_ge(decode, 6)
            nc.vector.tensor_tensor(src_abs[:], turned[:], place[:], ALU.add).then_inc(decode, 1)
            dve.wait_ge(decode, 7)

            dve.wait_ge(limit_in, 16)
            nc.vector.tensor_tensor(turned[:], limit[:, 0, :], src_abs[:], ALU.subtract).then_inc(check, 1)
            nc.vector.tensor_tensor(place[:], src_abs[:], limit[:, 1, :], ALU.subtract).then_inc(check, 1)
            dve.wait_ge(check, 2)
            nc.vector.tensor_tensor(turned[:], turned[:], place[:], ALU.max).then_inc(check, 1)
            dve.wait_ge(check, 3)
            nc.vector.tensor_reduce(outside[:], turned[:], AX.X, ALU.max).then_inc(check, 1)
            dve.wait_ge(check, 4)
            dve.wait_ge(late_ready, 1)
            nc.vector.tensor_tensor(outside[:], outside[:], late[:, 0:1], ALU.max).then_inc(check, 1)

            def low(t, slot, u):
                dve.wait_ge(hi_ready, t + (u + 1))
                if u % BATCH == 0:
                    dve.wait_ge(gathered[u // BATCH], t * (16 // 2) + (16 * BATCH))
                nc.vector.scalar_tensor_tensor(
                    m_lo[:, u % MRING, :], ring[:, bass.ds((slot + u) * FEAT, FEAT)],
                    wgt[:, bass.ds(t + u, 1)], m_hi[:, u % MRING, :], ALU.mult, ALU.subtract).then_inc(col_ready, 1)

            def select(c, slot, lo, hi):
                return nc.vector.tensor_scalar(sel[:, slot, 0:hi - lo], iota[:, lo:hi],
                                               src_abs[:, bass.ds(c, 1)], None, ALU.is_equal)

            def next_rows(t, slot):
                nc.vector.tensor_copy(ring_idx[:, bass.ds(slot, BODY)],
                                      row_idx[:, bass.ds(t + RING, BODY)]).then_inc(idx_ready, 1)

            def copy_bank(k):
                lo, hi = banks[done[k]]
                dve.wait_ge(col_summed, last_col[done[k]] + 1)
                if k < 2:
                    dve.wait_ge(stored[k], 16 * len(range(k, UNITS, STAGE)))
                else:
                    dve.wait_ge(sums_turned, k - 1)
                nc.vector.tensor_copy(stage[:, k % 2, 0:hi - lo], acc[:, lo:hi]).then_inc(sums_copied, 1)

            def out_bank(k):
                lo, hi = banks[done[k]]
                dve.wait_ge(sums_turned, k + 1)
                xs = x_sb[:, lo // P:hi // P, :].rearrange("p g f -> p (g f)")
                nc.vector.tensor_tensor(xs, psum[:, SPARE[k % 2], 0:hi - lo], xs, ALU.add).then_inc(out_ready, 1)

            dve.wait_ge(outside_t, 1)
            nc.vector.tensor_reduce(long_f[:], psum[0:1, 3, 0:P], AX.X, ALU.max).then_inc(check, 1)
            dve.wait_ge(check, CHECKED + 1)
            nc.vector.tensor_scalar(long_i[:], long_f[:], 0.0, None, ALU.is_gt).then_inc(long_ready, 1)
            dve.wait_ge(long_ready, 1)

            is_long = dve.value_load(long_i[0:1, 0:1], min_val=0, max_val=1)
            with dve.If(is_long > 0):
                for lap in range(LAPS):
                    start = lap * LAP_BODIES

                    def long_body(body, first):
                        t, slot = body * BODY, (body - lap * LAP_BODIES) * BODY
                        for u in range(BODY):
                            low(t, slot, u)
                            for p, (lo, hi) in enumerate(banks):
                                n = u * len(banks) + p
                                if not (first and n < SRING):
                                    dve.wait_ge(pass_summed, body * (BODY * len(banks)) + (n - SRING + 1))
                                select(t + u, n % SRING, lo, hi).then_inc(sel_ready, 1)
                        if lap < LAPS - 1:
                            next_rows(t, slot)

                    if lap == 0:
                        long_body(0, True)
                        start = 1
                    with dve.Fori(start, (lap + 1) * LAP_BODIES) as body:
                        long_body(body, False)
                dve.wait_ge(col_summed, COLS)
                for k in range(len(banks)):
                    copy_bank(k)
                    out_bank(k)
            with dve.Else():
                copied = turned_out = 0
                for c, (lo, hi) in enumerate(window):
                    if c in dve_cols:
                        n = dve_cols.index(c)
                        if n >= SRING:
                            dve.wait_ge(col_summed, dve_cols[n - SRING] + 1)
                        select(c, n % SRING, lo, hi).then_inc(sel_ready, 1)
                    low(c // BODY * BODY, c // BODY * BODY % RING, c % BODY)
                    if c % BODY == BODY - 1 and c < COLS - RING:
                        next_rows(c - BODY + 1, (c - BODY + 1) % RING)
                    if copied < len(banks) and last_col[done[copied]] + COPY_LAG <= c:
                        copy_bank(copied)
                        copied += 1
                    if turned_out < copied and last_col[done[turned_out]] + OUT_LAG <= c:
                        out_bank(turned_out)
                        turned_out += 1
                for k in range(turned_out, len(banks)):
                    if k >= copied:
                        copy_bank(k)
                    out_bank(k)


_INS = ["x", "src", "dst", "edge_type_32", "edge_weight", "L0_gnn_weight_relation", "L0_gnn_root"]


def kernel(**inputs):
    import concourse.bacc as bacc
    from concourse.bass_utils import run_bass_kernel_spmd as run

    nc = bacc.Bacc("TRN2", target_bir_lowering=False, num_devices=1)
    arrays, args = {}, []
    for name in _INS:
        a = np.ascontiguousarray(inputs[name])
        arrays[f"in_{name}"] = a
        args.append(nc.dram_tensor(f"in_{name}", a.shape, mybir.dt.from_np(a.dtype), kind="ExternalInput").ap())
    arrays["limits"] = np.array([[lo for lo, _ in windows()], [hi - 1 for _, hi in windows()]], np.float32)
    args.append(nc.dram_tensor("limits", arrays["limits"].shape, F32, kind="ExternalInput").ap())
    out = nc.dram_tensor("out_0", (NODES, FEAT), F32, kind="ExternalOutput").ap()
    build(nc, *args, out)
    return run(nc, [arrays], core_ids=[0]).results[0]["out_0"]
```
